# Optimizing a Trainium2 kernel written in Bass

```python
import numpy as np
import jax
import jax.numpy as jnp

def _softmax(x, axis=-1):
    return jax.nn.softmax(x, axis=axis)

def _gelu(x):
    return jax.nn.gelu(x, approximate=True)

def _silu(x):
    return jax.nn.silu(x)

def _sigmoid(x):
    return jax.nn.sigmoid(x)

def _layernorm(x, axis=-1, eps=1e-05):
    m = jnp.mean(x, axis=axis, keepdims=True)
    v = jnp.var(x, axis=axis, keepdims=True)
    return (x - m) / jnp.sqrt(v + eps)

def _scatter_add(tgt, idx, src, axis=0):
    return tgt.at[idx].add(src)

def _segment_sum(src, seg, n):
    return jax.ops.segment_sum(src, seg, n)
kernel_name = 'mk_prb_d1_jaxref_r8_6e9a6e'

def setup_inputs(seed: int=0):
    np.random.seed(seed)
    _w = jnp.asarray

    def _L0_attn_setup():
        import jax, jax.numpy as jnp
        import numpy as np
        H = 16
        CHUNK = 64
        EPS = 1e-05

        def _forward(x, wq, wk, wv, wo, fq1_w, fq1_b, fq2_w, fq2_b, fk1_w, fk1_b, fk2_w, fk2_b, norm_w):
            B, L, D = x.shape
            dk = D // H

            def proj(w):
                return (x @ w.T).reshape(B, L, H, dk).transpose(0, 2, 1, 3)
            q, k, v = (proj(wq), proj(wk), proj(wv))
            q = (q @ fq1_w.T + fq1_b) * (q @ fq2_w.T + fq2_b)
            k = (k @ fk1_w.T + fk1_b) * (k @ fk2_w.T + fk2_b)
            scale = dk ** (-0.5)
            n = L // CHUNK
            qc = q.reshape(B, H, n, CHUNK, dk) * scale
            kc = k.reshape(B, H, n, CHUNK, dk)
            vc = v.reshape(B, H, n, CHUNK, dk)
            kv = jnp.einsum('bhncd,bhnce->bhnde', kc, vc)
            kv = jnp.cumsum(kv, axis=2)
            kv = jnp.concatenate([jnp.zeros_like(kv[:, :, :1]), kv[:, :, :-1]], axis=2)
            inter = jnp.einsum('bhncd,bhnde->bhnce', qc, kv)
            s = jnp.einsum('bhncd,bhnmd->bhncm', qc, kc)
            mask = jnp.tril(jnp.ones((CHUNK, CHUNK), bool))
            s = jnp.where(mask, s, 0.0)
            intra = jnp.einsum('bhncm,bhnmd->bhncd', s, vc)
            o = (inter + intra).reshape(B, H, L, dk)
            o = o * jax.lax.rsqrt(jnp.mean(o * o, axis=-1, keepdims=True) + EPS) * norm_w
            o = o.transpose(0, 2, 1, 3).reshape(B, L, D)
            return o @ wo.T
        key = jax.random.key(seed)
        ks = jax.random.split(key, 16)
        B, L, D = (2, 512, 256)
        dk = D // H
        g = 2 ** (-2.5)

        def xav(k, n):
            lim = g * np.sqrt(6.0 / (2 * n))
            return jax.random.uniform(k, (n, n), jnp.float32, -lim, lim)
        return {'x': jax.random.normal(ks[0], (B, L, D), jnp.float32), 'wq': xav(ks[1], D), 'wk': xav(ks[2], D), 'wv': xav(ks[3], D), 'wo': xav(ks[4], D), 'fq1_w': xav(ks[5], dk), 'fq1_b': jnp.zeros((dk,), jnp.float32), 'fq2_w': xav(ks[6], dk), 'fq2_b': jnp.zeros((dk,), jnp.float32), 'fk1_w': xav(ks[7], dk), 'fk1_b': jnp.zeros((dk,), jnp.float32), 'fk2_w': xav(ks[8], dk), 'fk2_b': jnp.zeros((dk,), jnp.float32), 'norm_w': jnp.ones((dk,), jnp.float32)}
    _L0_attn_in = _L0_attn_setup()

    def _L0_ffn_setup():
        import jax, jax.numpy as jnp
        import numpy as np
        TOP_P = 0.9
        S, B, H, I, E = (256, 4, 256, 512, 8)

        def _top_p_weights(probs, top_p):
            order = jnp.argsort(-probs, axis=-1)
            sp = jnp.take_along_axis(probs, order, axis=-1)
            cum = jnp.cumsum(sp, axis=-1)
            exceed = cum > top_p
            first_idx = jnp.argmax(exceed, axis=-1)
            first = jnp.arange(probs.shape[-1])[None, :] == first_idx[:, None]
            keep = ~exceed | first
            kept = jnp.where(keep, sp, 0.0)
            t_idx = jnp.arange(probs.shape[0])[:, None]
            return jnp.zeros_like(probs).at[t_idx, order].set(kept)
        key = jax.random.key(seed)
        ks = jax.random.split(key, 5)
        scale = 0.02
        return {'hidden_states': jax.random.normal(ks[0], (S, B, H), dtype=jnp.float32), 'router_w': jax.random.normal(ks[1], (E, H), dtype=jnp.float32) * scale, 'gate_w': jax.random.normal(ks[2], (E, I, H), dtype=jnp.float32) * scale, 'up_w': jax.random.normal(ks[3], (E, I, H), dtype=jnp.float32) * scale, 'down_w': jax.random.normal(ks[4], (E, H, I), dtype=jnp.float32) * scale}
    _L0_ffn_in = _L0_ffn_setup()
    _d = {'L0_attn_x': _L0_attn_in['x'], 'L0_attn_wq': _L0_attn_in['wq'], 'L0_attn_wk': _L0_attn_in['wk'], 'L0_attn_wv': _L0_attn_in['wv'], 'L0_attn_wo': _L0_attn_in['wo'], 'L0_attn_fq1_w': _L0_attn_in['fq1_w'], 'L0_attn_fq1_b': _L0_attn_in['fq1_b'], 'L0_attn_fq2_w': _L0_attn_in['fq2_w'], 'L0_attn_fq2_b': _L0_attn_in['fq2_b'], 'L0_attn_fk1_w': _L0_attn_in['fk1_w'], 'L0_attn_fk1_b': _L0_attn_in['fk1_b'], 'L0_attn_fk2_w': _L0_attn_in['fk2_w'], 'L0_attn_fk2_b': _L0_attn_in['fk2_b'], 'L0_attn_norm_w': _L0_attn_in['norm_w'], 'L0_ffn_router_w': _L0_ffn_in['router_w'], 'L0_ffn_gate_w': _L0_ffn_in['gate_w'], 'L0_ffn_up_w': _L0_ffn_in['up_w'], 'L0_ffn_down_w': _L0_ffn_in['down_w']}
    _x0 = _d['L0_attn_x']
    _d['L0_attn_x'] = jax.random.normal(jax.random.fold_in(jax.random.key(seed), 1), (16, 256, 256), dtype=_x0.dtype)
    del _x0
    return _d

def reference(L0_attn_x, L0_attn_wq, L0_attn_wk, L0_attn_wv, L0_attn_wo, L0_attn_fq1_w, L0_attn_fq1_b, L0_attn_fq2_w, L0_attn_fq2_b, L0_attn_fk1_w, L0_attn_fk1_b, L0_attn_fk2_w, L0_attn_fk2_b, L0_attn_norm_w, L0_ffn_router_w, L0_ffn_gate_w, L0_ffn_up_w, L0_ffn_down_w):

    def _L0_attn_ref(x, wq, wk, wv, wo, fq1_w, fq1_b, fq2_w, fq2_b, fk1_w, fk1_b, fk2_w, fk2_b, norm_w):
        import jax, jax.numpy as jnp
        import numpy as np
        H = 16
        CHUNK = 64
        EPS = 1e-05

        def _forward(x, wq, wk, wv, wo, fq1_w, fq1_b, fq2_w, fq2_b, fk1_w, fk1_b, fk2_w, fk2_b, norm_w):
            B, L, D = x.shape
            dk = D // H

            def proj(w):
                return (x @ w.T).reshape(B, L, H, dk).transpose(0, 2, 1, 3)
            q, k, v = (proj(wq), proj(wk), proj(wv))
            q = (q @ fq1_w.T + fq1_b) * (q @ fq2_w.T + fq2_b)
            k = (k @ fk1_w.T + fk1_b) * (k @ fk2_w.T + fk2_b)
            scale = dk ** (-0.5)
            n = L // CHUNK
            qc = q.reshape(B, H, n, CHUNK, dk) * scale
            kc = k.reshape(B, H, n, CHUNK, dk)
            vc = v.reshape(B, H, n, CHUNK, dk)
            kv = jnp.einsum('bhncd,bhnce->bhnde', kc, vc)
            kv = jnp.cumsum(kv, axis=2)
            kv = jnp.concatenate([jnp.zeros_like(kv[:, :, :1]), kv[:, :, :-1]], axis=2)
            inter = jnp.einsum('bhncd,bhnde->bhnce', qc, kv)
            s = jnp.einsum('bhncd,bhnmd->bhncm', qc, kc)
            mask = jnp.tril(jnp.ones((CHUNK, CHUNK), bool))
            s = jnp.where(mask, s, 0.0)
            intra = jnp.einsum('bhncm,bhnmd->bhncd', s, vc)
            o = (inter + intra).reshape(B, H, L, dk)
            o = o * jax.lax.rsqrt(jnp.mean(o * o, axis=-1, keepdims=True) + EPS) * norm_w
            o = o.transpose(0, 2, 1, 3).reshape(B, L, D)
            return o @ wo.T
        return _forward(x, wq, wk, wv, wo, fq1_w, fq1_b, fq2_w, fq2_b, fk1_w, fk1_b, fk2_w, fk2_b, norm_w)

    def _L0_ffn_ref(hidden_states, router_w, gate_w, up_w, down_w):
        import jax, jax.numpy as jnp
        import numpy as np
        TOP_P = 0.9
        S, B, H, I, E = (256, 4, 256, 512, 8)

        def _top_p_weights(probs, top_p):
            order = jnp.argsort(-probs, axis=-1)
            sp = jnp.take_along_axis(probs, order, axis=-1)
            cum = jnp.cumsum(sp, axis=-1)
            exceed = cum > top_p
            first_idx = jnp.argmax(exceed, axis=-1)
            first = jnp.arange(probs.shape[-1])[None, :] == first_idx[:, None]
            keep = ~exceed | first
            kept = jnp.where(keep, sp, 0.0)
            t_idx = jnp.arange(probs.shape[0])[:, None]
            return jnp.zeros_like(probs).at[t_idx, order].set(kept)
        s, b, h = hidden_states.shape
        x = hidden_states.reshape(-1, h)
        probs = jax.nn.softmax(x @ router_w.T, axis=-1)
        w = _top_p_weights(probs, TOP_P)
        out = jnp.zeros_like(x)
        n_exp = router_w.shape[0]
        for e in range(n_exp):
            g = jax.nn.silu(x @ gate_w[e].T)
            u = x @ up_w[e].T
            y = g * u @ down_w[e].T
            out = out + y * w[:, e:e + 1]
        return out.reshape(s, b, h)
    x = L0_attn_x
    xn = _layernorm(x, axis=-1)
    x = x + _L0_attn_ref(xn, L0_attn_wq, L0_attn_wk, L0_attn_wv, L0_attn_wo, L0_attn_fq1_w, L0_attn_fq1_b, L0_attn_fq2_w, L0_attn_fq2_b, L0_attn_fk1_w, L0_attn_fk1_b, L0_attn_fk2_w, L0_attn_fk2_b, L0_attn_norm_w) + _L0_ffn_ref(xn, L0_ffn_router_w, L0_ffn_gate_w, L0_ffn_up_w, L0_ffn_down_w)
    return x

_drawn_inputs = setup_inputs


def setup_inputs(seed=0):
    import zlib

    import numpy as np

    out = dict(_drawn_inputs(seed))
    spreads = {'L0_attn_fq1_b': (0.0, 0.8),
     'L0_attn_fq2_b': (0.0, 0.78),
     'L0_attn_fk1_b': (0.0, 0.698),
     'L0_attn_fk2_b': (0.0, 0.8),
     'L0_attn_norm_w': (1.0, 0.6)}
    factors = {'L0_attn_wq': 8.0,
     'L0_attn_wk': 7.375,
     'L0_attn_wv': 5.176,
     'L0_attn_wo': 5.184,
     'L0_attn_fq1_w': 7.765,
     'L0_attn_fq2_w': 8.0,
     'L0_attn_fk1_w': 8.0,
     'L0_attn_fk2_w': 7.218,
     'L0_ffn_router_w': 8.0,
     'L0_ffn_gate_w': 6.546,
     'L0_ffn_up_w': 6.46,
     'L0_ffn_down_w': 6.469}
    for name, (base, spread) in spreads.items():
        noise = np.random.default_rng([zlib.crc32(name.encode()), seed]).standard_normal(out[name].shape)
        drawn = base * np.exp(spread * noise) if base else spread * noise
        out[name] = jnp.asarray(drawn.astype(out[name].dtype))
    for name, factor in factors.items():
        out[name] = (out[name] * factor).astype(out[name].dtype)
    return out
```

```python
from contextlib import ExitStack

import concourse.bass as bass
from concourse import mybir
from concourse.alu_op_type import AluOpType as ALU

F32 = mybir.dt.float32
F32R = mybir.dt.float32r
BF16 = mybir.dt.bfloat16
I32 = mybir.dt.int32
U32 = mybir.dt.uint32
ACT = mybir.ActivationFunctionType
X_AXIS = mybir.AxisListType.X

P = 128
NT = 4096
D = 256
KC = D // P
BLK = 512
NBLK = NT // BLK
TT = BLK // P
DK = 16
HH = P // DK
PAIRS = HH // 2
NE = 8
NI = 512
IC = NI // P
TOP_P = 0.9
LN_EPS = 1e-5
RMS_EPS = 1e-5
AUG = D + NE
FT = 256
SUB = FT // P
MAX_TILES = NT // FT
WE = KC * NI * 2 + IC * D
PIECES = 4
PW = WE // PIECES
NGROUP = 2 * 2 * PAIRS
DMA = 16


class Chain:

    def __init__(self, eng, sem, base=None):
        self.eng, self.sem, self.base, self.n = eng, sem, base, 0

    def link(self, ins):
        ins.then_inc(self.sem, 1)
        self.n += 1
        self.eng.wait_ge(self.sem, self.n if self.base is None else self.base + self.n)


def build(nc, x, wqk_nat, small, wvo, router, wffn, out):
    ctx = ExitStack()
    with ctx:
        def sb(name, shape, dt=F32):
            return ctx.enter_context(nc.sbuf_tensor(name, shape, dt))

        def ps(name, shape, dt=F32):
            return ctx.enter_context(nc.psum_tensor(name, shape, dt))

        def sem(name):
            return ctx.enter_context(nc.semaphore(name))

        x_blk = x.rearrange("(s t p) d -> s p t d", t=TT, p=P)
        out_blk = out.rearrange("(s t p) d -> s p t d", t=TT, p=P)
        table = nc.dram_tensor("gather_table", [NT, AUG], F32, kind="Internal").ap()
        table_blk = table.rearrange("(s t p) d -> s p t d", t=TT, p=P)

        ident = sb("ident", [P, P])
        head_mask = sb("head_mask", [P, HH, DK])
        head_mean = sb("head_mean", [P, P])
        causal = sb("causal", [P, P])
        before = sb("before", [P, P], BF16)
        ones_bf = sb("ones_bf", [P, P], BF16)
        lo_iota = sb("lo_iota", [P, P])
        hi_iota = sb("hi_iota", [P, NT // P])
        part = sb("part", [P, 1])
        lower_e = sb("lower_e", [P, NE, NE])
        parity = sb("parity", [P, 2])
        parity_b = sb("parity_b", [P, 2])
        eps = sb("eps", [P, 1])
        bq2 = sb("bq2", [P, 1])
        smalls = sb("smalls", [P, 4 * DK + 5])
        wqk_hi = sb("wqk_hi", [P, 4, KC, D], F32R)
        wqk_lo = sb("wqk_lo", [P, 4, KC, D], F32R)
        wvo_hi = sb("wvo_hi", [P, 2, KC, D], F32R)
        wvo_lo = sb("wvo_lo", [P, 2, KC, D], F32R)
        rt_raw = sb("rt_raw", [P, KC, NE])
        rt_hi = sb("rt_hi", [P, KC, NE], F32R)
        rt_lo = sb("rt_lo", [P, KC, NE], F32R)
        feat = sb("feat", [P, 4, P])
        w_raw = sb("w_raw", [P, WE])
        w_hi = [sb(f"w_hi{i}", [P, WE], F32R) for i in range(2)]
        w_lo = [sb(f"w_lo{i}", [P, WE], F32R) for i in range(2)]
        base = sb("base", [P, TT + 1, NE])
        from_end = sb("from_end", [P, TT])
        tile_no = sb("tile_no", [P, TT])
        idx_acc = sb("idx_acc", [P, NE, 2, NT // P])
        idx_all = sb("idx_all", [P, NE * (NT // P)], U32)
        n_tiles = sb("n_tiles", [1, NE], I32)

        ph1 = ExitStack()

        def sb1(name, shape, dt=F32):
            return ph1.enter_context(nc.sbuf_tensor(name, shape, dt))

        xa = sb1("xa", [P, TT, D])
        stats = sb1("stats", [P, TT, 6])
        mv = sb1("mv", [P, TT, 2])
        rstd_x = sb1("rstd_x", [P, TT])
        var_eps = sb1("var_eps", [P, TT])
        newton = sb1("newton", [P, TT])
        ln_x = sb1("ln_x", [P, TT])
        ln_o = sb1("ln_o", [P, 2, BLK])
        slot_i = sb1("slot_i", [P, TT, NE], I32)
        lo_i = sb1("lo_i", [P, TT, NE], I32)
        xna = sb1("xna", [P, TT, AUG])
        xT_hi = sb1("xT_hi", [P, KC, BLK], F32R)
        xT_lo = sb1("xT_lo", [P, KC, BLK], F32R)
        t2q = sb1("t2q", [P, 2, BLK])
        t2k = sb1("t2k", [P, 2, 2, BLK])
        q = sb1("q", [P, 2, BLK])
        kz = sb1("kz", [P, 2, 2, BLK])
        kf = sb1("kf", [P, 2, 2, P])
        k_tok = sb1("k_tok", [P, 2, 2, P])
        kv = sb1("kv", [P, 2, 2, P])
        vz = sb1("vz", [P, TT, 2 * PAIRS, 4, DK])
        s_sb = sb1("s_sb", [P, 2, 4, P])
        sq = sb1("sq", [P, 2, BLK])
        rstd_o = sb1("rstd_o", [P, 2, BLK])
        on = sb1("on", [P, 2, BLK])
        on_hi = sb1("on_hi", [P, 2, BLK], F32R)
        on_lo = sb1("on_lo", [P, 2, BLK], F32R)
        xr = sb1("xr", [P, TT, D])
        yout = sb1("yout", [P, TT, D])
        lg = sb1("lg", [P, TT, NE])
        mx = sb1("mx", [P, TT])
        ls = sb1("ls", [P, TT, NE])
        ex = sb1("ex", [P, TT, NE])
        sm = sb1("sm", [P, TT])
        pr = sb1("pr", [P, TT, NE])
        c_gt = sb1("c_gt", [P, TT, NE, NE])
        c_eq = sb1("c_eq", [P, TT, NE, NE])
        cum = sb1("cum", [P, TT, NE])
        keep = sb1("keep", [P, TT, NE])
        sel = sb1("sel", [P, TT, NE], BF16)
        slot = sb1("slot", [P, TT, NE])
        slot_lo = sb1("slot_lo", [P, TT, NE])
        slot_hi = sb1("slot_hi", [P, TT, NE])
        oh_lo = sb1("oh_lo", [P, TT * NE, P], BF16)
        oh_hi = sb1("oh_hi", [P, TT * NE, NT // P])
        oh_rhs = sb1("oh_rhs", [P, TT * NE, 2, NT // P], BF16)
        ph1.close()

        ph2 = ctx.enter_context(ExitStack())

        def sb2(name, shape, dt=F32):
            return ph2.enter_context(nc.sbuf_tensor(name, shape, dt))

        idx_f = sb2("idx_f", [P, NE, NT // P])
        cnt_i = sb2("cnt_i", [1, NE], I32)
        xg = sb2("xg", [P, SUB, AUG])
        g_idx = sb2("g_idx", [P, SUB], U32)
        s_idx = sb2("s_idx", [P, SUB], U32)
        gT_hi = sb2("gT_hi", [P, KC, FT], F32R)
        gT_lo = sb2("gT_lo", [P, KC, FT], F32R)
        sg = sb2("sg", [P, IC, FT])
        h = sb2("h", [P, IC, FT])
        h_hi = sb2("h_hi", [P, IC, FT], F32R)
        h_lo = sb2("h_lo", [P, IC, FT], F32R)
        ybuf = sb2("ybuf", [P, SUB, D])
        w_tok = sb2("w_tok", [P, (NE * MAX_TILES + 1) * SUB * NE])

        A = [ps(f"A{i}", [P, 512]) for i in range(4)]
        S = [ps(f"S{i}", [P, 512]) for i in range(2)]
        O = [ps(f"O{i}", [P, 512]) for i in range(2)]

        names = ("loads natural masks feat_ok fused_ps fused_ok split_ok setup_dve setup_act "
                 "x_in xn_ok xt_ps xhi_ok xlo_ok lg_ps lg_ok proj_ps t2_ok qk_ok v_ok kf_ok kt_ps kt_ok kv_ps kv_ok "
                 "s_ps s_ok pv_ps sq_ok ms_ps ro_ok var_ok rs0_ok ln_x_ok ln_o_ok on_ok onhi_ok onlo_ok wo_ps o_free xr_in yout_free y_ok "
                 "ls_ok ex_ok sel_ok rank_ps rank_ok slot_ok lo_ok oh_ok idx_ps idx_ok w_ok table_in "
                 "dve_step pool_step act_step tab_ok w_in wsplit w_free "
                 "gi_step gathered xg_free ghi_ok glo_ok gu_ps silu_ok h_free hhi_ok hlo_ok y_ps ya_ok yd_ok "
                 "wt_ok scattered pool_gate dve_gate pe_gate")
        sems = {n: sem(n) for n in names.split()}
        (loads, natural, masks, feat_ok, fused_ps, fused_ok, split_ok, setup_dve, setup_act,
         x_in, xn_ok, xt_ps, xhi_ok, xlo_ok, lg_ps, lg_ok, proj_ps, t2_ok, qk_ok, v_ok, kf_ok, kt_ps, kt_ok, kv_ps, kv_ok,
         s_ps, s_ok, pv_ps, sq_ok, ms_ps, ro_ok, var_ok, rs0_ok, ln_x_ok, ln_o_ok, on_ok, onhi_ok, onlo_ok, wo_ps, o_free, xr_in, yout_free, y_ok,
         ls_ok, ex_ok, sel_ok, rank_ps, rank_ok, slot_ok, lo_ok, oh_ok, idx_ps, idx_ok, w_ok, table_in,
         dve_step, pool_step, act_step, tab_ok, w_in, wsplit, w_free,
         gi_step, gathered, xg_free, ghi_ok, glo_ok, gu_ps, silu_ok, h_free, hhi_ok, hlo_ok, y_ps, ya_ok, yd_ok,
         wt_ok, scattered, pool_gate, dve_gate, pe_gate) = [sems[n] for n in names.split()]

        nat = w_raw[:, 0:2 * KC * D].rearrange("p (m c k) -> p m c k", m=2, c=KC)
        vo_raw = w_raw[:, 2 * KC * D:4 * KC * D].rearrange("p (m c k) -> p m c k", m=2, c=KC)
        down0 = 2 * KC * NI

        def bank_gu(ic):
            return (A[1], A[2], A[3], S[0])[ic]

        block = ctx.enter_context(nc.Block())

        @block.sync
        def _(sp):
            sp.dma_start(xa[:, :, :], x_blk[0]).then_inc(x_in, DMA)
            sp.dma_start(smalls[:, :], small).then_inc(loads, DMA)
            sp.dma_start(rt_raw[:, :, :], router).then_inc(loads, DMA)
            sp.dma_start(nat, wqk_nat).then_inc(natural, DMA)
            sp.dma_start(vo_raw, wvo).then_inc(loads, DMA)
            sp.wait_ge(split_ok, 2)
            sp.dma_start(w_raw[:, :], wffn[0]).then_inc(w_in, DMA)

            def block_step(s, last):
                if not last:
                    sp.wait_ge(xn_ok, s + 1)
                    sp.dma_start(xa[:, :, :], x_blk[s + 1]).then_inc(x_in, DMA)
                sp.wait_ge(o_free, 2 * s + 2)
                sp.dma_start(xr[:, :, :], x_blk[s]).then_inc(xr_in, DMA)
                sp.wait_ge(w_ok, s + 1)
                sp.dma_start(table_blk[s], xna[:, :, :]).then_inc(table_in, DMA)
                sp.wait_ge(y_ok, 2 * s + 2)
                sp.dma_start(out_blk[s], yout[:, :, :]).then_inc(yout_free, DMA)

            with sp.Fori(0, NBLK - 1) as s:
                block_step(s, False)
            block_step(NBLK - 1, True)
            for e in range(1, NE):
                sp.wait_ge(wsplit, PIECES * e)
                sp.dma_start(w_raw[:, :], wffn[e]).then_inc(w_in, DMA)

        @block.gpsimd
        def _(pool):
            g = nc.gpsimd
            g.memset(ident[:, :], 0.0).then_inc(pool_step, 1)
            g.memset(head_mask[:, :, :], 1.0).then_inc(pool_step, 1)
            g.memset(causal[:, :], 1.0).then_inc(pool_step, 1)
            g.memset(before[:, :], 1.0).then_inc(pool_step, 1)
            g.memset(lower_e[:, :, :], 1.0).then_inc(pool_step, 1)
            pool.wait_ge(pool_step, 5)
            g.affine_select(out=ident[:, :], in_=ident[:, :], compare_op=ALU.not_equal, fill=1.0,
                            base=0, pattern=[[-1, P]], channel_multiplier=1).then_inc(pool_step, 1)
            g.affine_select(out=head_mask[:, :, :], in_=head_mask[:, :, :], compare_op=ALU.is_ge, fill=0.0,
                            base=0, pattern=[[-DK, HH], [0, DK]], channel_multiplier=1).then_inc(pool_step, 1)
            g.affine_select(out=causal[:, :], in_=causal[:, :], compare_op=ALU.is_ge, fill=0.0,
                            base=0, pattern=[[1, P]], channel_multiplier=-1).then_inc(pool_step, 1)
            g.affine_select(out=before[:, :], in_=before[:, :], compare_op=ALU.is_ge, fill=0.0,
                            base=-1, pattern=[[1, P]], channel_multiplier=-1).then_inc(pool_step, 1)
            g.affine_select(out=lower_e[:, :, :], in_=lower_e[:, :, :], compare_op=ALU.is_ge, fill=0.0,
                            base=-1, pattern=[[1, NE], [-1, NE]], channel_multiplier=0).then_inc(pool_step, 1)
            pool.wait_ge(pool_step, 10)
            g.affine_select(out=head_mask[:, :, :], in_=head_mask[:, :, :], compare_op=ALU.is_ge, fill=0.0,
                            base=DK - 1, pattern=[[DK, HH], [0, DK]], channel_multiplier=-1).then_inc(pool_step, 1)
            pool.wait_ge(pool_step, 11)
            g.memset(ones_bf[:, :], 1.0)
            g.memset(eps[:, :], RMS_EPS)
            g.iota(lo_iota[:, :], pattern=[[1, P]], base=0, channel_multiplier=0, allow_small_or_imprecise_dtypes=True)
            g.iota(hi_iota[:, :], pattern=[[P, NT // P]], base=0, channel_multiplier=0,
                   allow_small_or_imprecise_dtypes=True)
            g.iota(part[:, :], pattern=[[0, 1]], base=0, channel_multiplier=1, allow_small_or_imprecise_dtypes=True)
            g.iota(from_end[:, :], pattern=[[-P, TT]], base=NT - 1, channel_multiplier=-1,
                   allow_small_or_imprecise_dtypes=True)
            g.iota(tile_no[:, :], pattern=[[1, TT]], base=0, channel_multiplier=0,
                   allow_small_or_imprecise_dtypes=True)
            g.memset(base[:, :, :], 0.0)
            g.memset(idx_acc[:, :, :, :], 0.0)
            g.memset(vz[:, :, :, :, :], 0.0)
            g.memset(yout[:, :, :], 0.0).then_inc(yout_free, DMA)
            g.tensor_scalar(head_mean[:, :], head_mask[:, :, :].rearrange("p h d -> p (h d)"), 1.0 / DK, None,
                            ALU.mult).then_inc(masks, 1)
            b_reg = pool.alloc_register("pool_base")
            pool.reg_mov(b_reg, 11)

            def block_step(s):
                chain = Chain(pool, pool_step, pool.snap(b_reg))
                for half in range(2):
                    pool.wait_ge(qk_ok, 6 * s + 3 * half + 3)
                    first = [kz[:, half, par, :].rearrange("p (b c m) -> p b c m", b=2, c=2)[:, :, 0, :]
                             for par in range(2)]
                    g.tensor_tensor(kf[:, half, :, :], first[0], first[1], ALU.add).then_inc(kf_ok, 1)
                pool.wait_ge(slot_ok, s + 1)
                pool.sem_inc(pool_gate, 1)
                g.tensor_scalar(oh_rhs[:, :, 0, :], oh_hi[:, :, :], part[:, 0:1], None, ALU.mult)
                for t in range(TT):
                    last = g.tensor_scalar(oh_rhs[:, t * NE:(t + 1) * NE, 1, :], oh_hi[:, t * NE:(t + 1) * NE, :],
                                           tile_no[:, t:t + 1], None, ALU.mult)
                last.then_inc(oh_ok, 1)
                pool.wait_ge(oh_ok, s + 1)
                pool.sem_inc(pool_gate, 1)
                chain.link(g.tensor_scalar(tile_no[:, :], tile_no[:, :], float(TT), None, ALU.add))
                for half in range(2):
                    pool.wait_ge(onhi_ok, 2 * s + half + 1)
                    g.tensor_tensor(on_lo[:, half, :], on[:, half, :], on_hi[:, half, :].bitcast(F32),
                                    ALU.subtract).then_inc(onlo_ok, 1)
                pool.reg_add(b_reg, b_reg, chain.n)

            with pool.Fori(0, NBLK - 1) as s:
                block_step(s)
            block_step(NBLK - 1)

            def split_piece(par, c0):
                raw = w_raw[:, bass.ds(c0, PW)]
                whi = w_hi[par][:, bass.ds(c0, PW)]
                wlo = w_lo[par][:, bass.ds(c0, PW)]
                link(g.tensor_copy(whi, raw))
                g.tensor_tensor(wlo, raw, whi.bitcast(F32), ALU.subtract).then_inc(wsplit, 1)

            step = pool.alloc_register("pool_steps")
            pool.reg_mov(step, b_reg)

            def link(ins):
                ins.then_inc(pool_step, 1)
                pool.wait_ge(pool_step, pool.snap(step) + 1)
                pool.reg_add(step, step, 1)
                pool.sem_inc(pool_gate, 1)

            pool.wait_ge(w_in, DMA)
            for piece in range(PIECES):
                split_piece(0, piece * PW)
            pool.wait_ge(tab_ok, 1)
            pool.wait_ge(table_in, DMA * NBLK)
            pool.wait_ge(yout_free, DMA * (NBLK + 1))

            done = pool.alloc_register("tiles_done")
            col1 = pool.alloc_register("col1")
            col2 = pool.alloc_register("col2")
            pieces = pool.alloc_register("pieces")
            piece_col = pool.alloc_register("piece_col")
            for r in (done, col1, col2):
                pool.reg_mov(r, 0)

            def gather(col):
                n = pool.snap(done)
                pool.wait_ge(xg_free, n + 1)
                pool.wait_ge(wt_ok, n + 1)
                pool.sem_inc(pool_gate, 1)
                link(g.tensor_copy(g_idx[:, :], idx_all[:, bass.ds(col, SUB)]))
                for sub in range(SUB):
                    pool.indirect_dma_start(
                        out=xg[:, sub, :], out_offset=None, in_=table,
                        in_offset=bass.IndirectOffsetOnAxis(ap=g_idx[:, sub:sub + 1], axis=0)).then_inc(gathered, DMA)

            def scatter():
                n = pool.snap(done)
                pool.wait_ge(ya_ok, n + 1)
                pool.wait_ge(yd_ok, n + 1)
                pool.wait_ge(scattered, (n + 1) * (SUB * DMA))
                pool.sem_inc(pool_gate, 1)
                link(g.tensor_copy(s_idx[:, :], idx_all[:, bass.ds(pool.snap(col2, min_val=0, max_val=NE * (NT // P) - SUB), SUB)]))
                add_rows()
                pool.reg_add(done, done, 1)

            def add_rows():
                for sub in range(SUB):
                    pool.indirect_dma_start(
                        out=out, out_offset=bass.IndirectOffsetOnAxis(ap=s_idx[:, sub:sub + 1], axis=0),
                        in_=ybuf[:, sub, :], in_offset=None, compute_op=ALU.add).then_inc(scattered, DMA)

            pool.wait_ge(ya_ok, 2)
            link(g.tensor_copy(s_idx[:, :], idx_all[:, 0:SUB]))
            add_rows()

            with pool.Fori(0, NE // 2) as ep:
                for par in range(2):
                    pool.reg_mov(pieces, PIECES)
                    if par == 1:
                        with pool.If(ep > NE // 2 - 2):
                            pool.reg_mov(pieces, 0)
                        pool.sem_inc(pool_gate, 1)
                    n = pool.value_load(n_tiles[0:1, bass.ds(ep * 2 + par, 1)], min_val=1, max_val=MAX_TILES)
                    with pool.Fori(0, n) as j:
                        col = pool.snap(ep * (2 * NT // P) + (par * (NT // P)) + j * SUB)
                        gather(col)
                        scatter()
                        pool.reg_mov(col2, col1)
                        pool.reg_mov(col1, col)
                        with pool.If(j < pool.snap(pieces)):
                            pool.wait_ge(w_free, ep * 2 + (par + 1))
                            pool.wait_ge(w_in, (ep * 2 + (par + 2)) * DMA)
                            pool.sem_inc(pool_gate, 1)
                            pool.reg_mov(piece_col, j * PW)
                            split_piece(1 - par, pool.snap(piece_col, min_val=0, max_val=(PIECES - 1) * PW))
                        pool.sem_inc(pool_gate, 1)
                    for piece in range(1, PIECES):
                        with pool.If(n + PIECES - pool.snap(pieces) < piece + 1):
                            pool.wait_ge(w_free, ep * 2 + (par + 1))
                            pool.wait_ge(w_in, (ep * 2 + (par + 2)) * DMA)
                            pool.sem_inc(pool_gate, 1)
                            split_piece(1 - par, piece * PW)
                        pool.sem_inc(pool_gate, 1)
            gather(0)
            scatter()
            pool.reg_mov(col2, col1)
            scatter()
            pool.wait_ge(scattered, (pool.snap(done) + 1) * (SUB * DMA))

        @block.scalar
        def _(act):
            a = nc.scalar
            for f in range(4):
                act.wait_ge(fused_ps, f + 1)
                a.activation(wqk_hi[:, f, :, :].rearrange("p c n -> p (c n)"), A[f][:, :], ACT.Copy).then_inc(setup_act, 1)

            def token_rstd(s):
                act.wait_ge(var_ok, s + 1)
                a.activation(ln_x[:, :], var_eps[:, :], ACT.Ln).then_inc(ln_x_ok, 1)
                act.wait_ge(ln_x_ok, s + 1)
                a.activation(rstd_x[:, :], ln_x[:, :], ACT.Exp, scale=-0.5).then_inc(rs0_ok, 1)

            def head_rstd(s, half):
                act.wait_ge(ms_ps, 2 * s + half + 1)
                a.activation(ln_o[:, half, :], (A[0] if half == 0 else A[2])[:, :], ACT.Ln, bias=eps[:, 0:1]).then_inc(ln_o_ok, 1)
                act.wait_ge(ln_o_ok, 2 * s + half + 1)
                a.activation(rstd_o[:, half, :], ln_o[:, half, :], ACT.Exp, scale=-0.5).then_inc(ro_ok, 1)

            def front(s):
                for c in range(KC):
                    act.wait_ge(xt_ps, KC * s + c + 1)
                    a.activation(xT_hi[:, c, :], A[c][:, :], ACT.Copy).then_inc(xhi_ok, 1)

            def block_step(s, last):
                for half in range(2):
                    act.wait_ge(proj_ps, 6 * s + 2 * half + 1)
                    if not last or True:
                        a.activation(t2q[:, half, :], A[1][:, :], ACT.Identity, bias=bq2[:, 0:1],
                                     scale=DK ** -0.5).then_inc(t2_ok, 1)
                    act.wait_ge(proj_ps, 6 * s + 2 * half + 2)
                    for par in range(2):
                        a.activation(t2k[:, half, par, :], A[3][:, :], ACT.Identity, bias=parity_b[:, par:par + 1],
                                     scale=parity[:, par:par + 1]).then_inc(t2_ok, 1)
                for i in range(2):
                    act.wait_ge(proj_ps, 6 * s + 5 + i)
                    for j in range(2):
                        o = vz[:, 2 * i + j, :, 0:4:3, :]
                        last_v = a.activation(o, A[i][:, j * D:(j + 1) * D].rearrange("p (g e d) -> p g e d", e=2, d=DK),
                                              ACT.Copy)
                    last_v.then_inc(v_ok, 1)
                act.wait_ge(kt_ps, s + 1)
                a.activation(k_tok[:, :, :, :].rearrange("p a b m -> p (a b m)"), A[2][:, :], ACT.Copy).then_inc(kt_ok, 1)
                act.wait_ge(ls_ok, s + 1)
                a.activation(ex[:, :, :], ls[:, :, :], ACT.Exp).then_inc(ex_ok, 1)
                for half in range(2):
                    act.wait_ge(pv_ps, NGROUP * s + NGROUP // 2 * (half + 1))
                    a.activation(sq[:, half, :], O[half][:, :], ACT.Square).then_inc(sq_ok, 1)
                    if half == 1 and not last:
                        front(s + 1)
                    head_rstd(s, half)
                    act.wait_ge(on_ok, 2 * s + half + 1)
                    a.activation(on_hi[:, half, :], on[:, half, :], ACT.Copy).then_inc(onhi_ok, 1)
                    if half == 0 and not last:
                        token_rstd(s + 1)

            token_rstd(0)
            front(0)
            with act.Fori(0, NBLK - 1) as s:
                block_step(s, False)
            block_step(NBLK - 1, True)

            done = act.alloc_register("act_tiles")
            act.reg_mov(done, 0)

            def tokens_hi(n):
                act.wait_ge(xg_free, n + 2)
                a.activation(gT_hi[:, :, :].rearrange("p c t -> p (c t)"), A[0][:, :], ACT.Copy).then_inc(ghi_ok, 1)

            tokens_hi(0)
            with act.Fori(0, NE // 2) as ep:
                for par in range(2):
                    n = act.value_load(n_tiles[0:1, bass.ds(ep * 2 + par, 1)], min_val=1, max_val=MAX_TILES)
                    with act.Fori(0, n):
                        t = act.snap(done, min_val=0, max_val=NE * MAX_TILES - 1)
                        for ic in range(IC):
                            act.wait_ge(gu_ps, t * IC + (ic + 1))
                            a.activation(sg[:, ic, :], bank_gu(ic)[:, 0:FT], ACT.Silu).then_inc(silu_ok, 1)
                            act.wait_ge(h_free, t * IC + (ic + 1 + IC))
                            a.activation(h_hi[:, ic, :], h[:, ic, :], ACT.Copy).then_inc(hhi_ok, 1)
                        tokens_hi(t + 1)
                        act.wait_ge(y_ps, t * SUB + 1)
                        act.wait_ge(scattered, (t + 3) * (SUB * DMA))
                        a.activation(ybuf[:, 0, :], O[0][:, 0:D], ACT.Copy,
                                     scale=w_tok[:, bass.ds(t * (SUB * NE) + (ep * 2 + par), 1)]).then_inc(ya_ok, 1)
                        act.reg_add(done, done, 1)

        @block.vector
        def _(dve):
            v = nc.vector
            c0 = Chain(dve, setup_dve)
            dve.wait_ge(loads, 3 * DMA)
            dve.wait_ge(masks, 1)
            for f in range(4):
                v.tensor_tensor(feat[:, f, :].rearrange("p (h d) -> p h d", h=HH), head_mask[:, :, :],
                                smalls[:, f * DK:(f + 1) * DK].unsqueeze(1).to_broadcast([P, HH, DK]),
                                ALU.mult).then_inc(feat_ok, 1)
            for par in range(2):
                last = v.tensor_reduce(parity[:, par:par + 1], head_mask[:, par:HH:2, 0:1].rearrange("p h d -> p d h"),
                                       axis=X_AXIS, op=ALU.add)
            c0.link(last)
            v.tensor_scalar(parity_b[:, :], parity[:, :], smalls[:, 4 * DK + 3:4 * DK + 4], None, ALU.mult)
            v.tensor_scalar(bq2[:, :], smalls[:, 4 * DK + 1:4 * DK + 2], DK ** -0.5, None, ALU.mult)
            for c in range(KC):
                last = v.tensor_scalar(vo_raw[:, 1, c, :], vo_raw[:, 1, c, :], smalls[:, 4 * DK + 4:4 * DK + 5], None,
                                       ALU.mult)
            c0.link(last)
            v.tensor_copy(wvo_hi[:, :, :, :], vo_raw)
            c0.link(v.tensor_copy(rt_hi[:, :, :], rt_raw[:, :, :]))
            v.tensor_tensor(wvo_lo[:, :, :, :], vo_raw, wvo_hi[:, :, :, :].bitcast(F32), ALU.subtract).then_inc(split_ok, 1)
            v.tensor_tensor(rt_lo[:, :, :], rt_raw[:, :, :], rt_hi[:, :, :].bitcast(F32), ALU.subtract)
            for f in range(4):
                dve.wait_ge(setup_act, f + 1)
                last = v.tensor_tensor(wqk_lo[:, f, :, :].rearrange("p c n -> p (c n)"), A[f][:, :],
                                       wqk_hi[:, f, :, :].rearrange("p c n -> p (c n)").bitcast(F32), ALU.subtract)
                last.then_inc(fused_ok, 1)
            v.memset(mx[:, :], 0.0).then_inc(o_free, 2)
            chain_reg = dve.alloc_register("dve_base")
            dve.reg_mov(chain_reg, 0)

            def norm_stats(s, chain):
                dve.wait_ge(x_in, DMA * s + DMA)
                for t in range(TT):
                    last = v.bn_stats(stats[:, t, :], xa[:, t, :])
                chain.link(last)
                dve.sem_inc(dve_gate, 1)
                for t in range(TT):
                    last = v.bn_aggr(mv[:, t, :], stats[:, t, :])
                chain.link(last)
                v.tensor_scalar(var_eps[:, :], mv[:, :, 1], LN_EPS, None, ALU.add).then_inc(var_ok, 1)

            def norm_refine(s, chain):
                dve.wait_ge(rs0_ok, s + 1)
                chain.link(v.tensor_tensor(newton[:, :], rstd_x[:, :], rstd_x[:, :], ALU.mult))
                chain.link(v.tensor_tensor(newton[:, :], newton[:, :], var_eps[:, :], ALU.mult))
                chain.link(v.tensor_scalar(newton[:, :], newton[:, :], -0.5, 1.5, ALU.mult, ALU.add))
                chain.link(v.tensor_tensor(rstd_x[:, :], rstd_x[:, :], newton[:, :], ALU.mult))

            def norm_apply(s, first=False):
                if not first:
                    dve.wait_ge(table_in, DMA * s)
                    dve.wait_ge(xt_ps, KC * s)
                for t in range(TT):
                    last = v.tensor_scalar(xna[:, t, 0:D], xa[:, t, :], mv[:, t, 0:1], rstd_x[:, t:t + 1],
                                           ALU.subtract, ALU.mult)
                last.then_inc(xn_ok, 1)

            def front_tail(s):
                for c in range(KC):
                    dve.wait_ge(xhi_ok, KC * s + c + 1)
                    v.tensor_tensor(xT_lo[:, c, :], A[c][:, :], xT_hi[:, c, :].bitcast(F32), ALU.subtract).then_inc(xlo_ok, 1)

            def logits_copy(s, chain):
                dve.wait_ge(lg_ps, s + 1)
                v.tensor_copy(lg[:, :, :].rearrange("p t e -> p (t e)"), A[3][:, 0:TT * NE]).then_inc(lg_ok, 1)

            def softmax_head(s, chain):
                dve.wait_ge(lg_ok, s + 1)
                chain.link(v.tensor_reduce(mx[:, :], lg[:, :, :], axis=X_AXIS, op=ALU.max))
                v.tensor_tensor(ls[:, :, :], lg[:, :, :], mx[:, :].unsqueeze(2).to_broadcast([P, TT, NE]),
                                ALU.subtract).then_inc(ls_ok, 1)

            def softmax_tail(s, chain):
                dve.wait_ge(ex_ok, s + 1)
                chain.link(v.tensor_reduce(sm[:, :], ex[:, :, :], axis=X_AXIS, op=ALU.add))
                chain.link(v.reciprocal(sm[:, :], sm[:, :]))
                chain.link(v.tensor_tensor(pr[:, :, :], ex[:, :, :], sm[:, :].unsqueeze(2).to_broadcast([P, TT, NE]),
                                           ALU.mult))

            def ranked_before(chain):
                pf = pr[:, :, :].unsqueeze(2).to_broadcast([P, TT, NE, NE])
                pe = pr[:, :, :].unsqueeze(3).to_broadcast([P, TT, NE, NE])
                v.tensor_tensor(c_gt[:, :, :, :], pf, pe, ALU.is_gt)
                chain.link(v.tensor_tensor(c_eq[:, :, :, :], pf, pe, ALU.is_equal))
                chain.link(v.tensor_tensor(c_eq[:, :, :, :], c_eq[:, :, :, :],
                                           lower_e[:, :, :].unsqueeze(1).to_broadcast([P, TT, NE, NE]), ALU.mult))
                chain.link(v.tensor_tensor(c_gt[:, :, :, :], c_gt[:, :, :, :], c_eq[:, :, :, :], ALU.add))
                chain.link(v.tensor_tensor(c_gt[:, :, :, :], c_gt[:, :, :, :], pf, ALU.mult))

            def choose(s, chain):
                chain.link(v.tensor_reduce(cum[:, :, :], c_gt[:, :, :, :], axis=X_AXIS, op=ALU.add))
                chain.link(v.tensor_scalar(keep[:, :, :], cum[:, :, :], TOP_P, None, ALU.is_le))
                v.tensor_copy(sel[:, :, :], keep[:, :, :]).then_inc(sel_ok, 1)
                v.tensor_tensor(xna[:, :, D:AUG], pr[:, :, :], keep[:, :, :], ALU.mult).then_inc(w_ok, 1)

            def slots(s, chain):
                dve.wait_ge(rank_ps, s + 1)
                for t in range(TT):
                    chain.link(v.tensor_tensor(base[:, t + 1, :], base[:, t, :],
                                               A[2][:, TT * NE + t * NE:TT * NE + (t + 1) * NE], ALU.add))
                v.tensor_tensor(slot[:, :, :], A[2][:, 0:TT * NE].rearrange("p (t e) -> p t e", t=TT),
                                base[:, 0:TT, :], ALU.add).then_inc(rank_ok, 1)
                chain.link(v.tensor_scalar(keep[:, :, :], keep[:, :, :], -1.0, 1.0, ALU.mult, ALU.add))
                chain.link(v.tensor_tensor(keep[:, :, :], keep[:, :, :],
                                           from_end[:, :].unsqueeze(2).to_broadcast([P, TT, NE]), ALU.mult))
                dve.wait_ge(rank_ok, s + 1)
                chain.link(v.tensor_tensor(slot[:, :, :], slot[:, :, :], keep[:, :, :], ALU.add))
                chain.link(v.tensor_copy(slot_i[:, :, :], slot[:, :, :]))
                chain.link(v.tensor_scalar(lo_i[:, :, :], slot_i[:, :, :], P - 1, None, ALU.bitwise_and))
                chain.link(v.tensor_copy(slot_lo[:, :, :], lo_i[:, :, :]))
                chain.link(v.tensor_tensor(slot_hi[:, :, :], slot[:, :, :], slot_lo[:, :, :], ALU.subtract))
                n = TT * NE
                hi = slot_hi[:, :, :].rearrange("p t e -> p (t e)")
                v.tensor_tensor(oh_hi[:, :, :], hi_iota[:, :].unsqueeze(1).to_broadcast([P, n, NT // P]),
                                hi.unsqueeze(2).to_broadcast([P, n, NT // P]), ALU.is_equal).then_inc(slot_ok, 1)
                v.tensor_scalar(from_end[:, :], from_end[:, :], float(-BLK), None, ALU.add)
                chain.link(v.tensor_copy(base[:, 0, :], base[:, TT, :]))

            def one_hot(s, t):
                ins = v.tensor_tensor(oh_lo[:, t * NE:(t + 1) * NE, :], lo_iota[:, :].unsqueeze(1).to_broadcast([P, NE, P]),
                                      slot_lo[:, t, :].unsqueeze(2).to_broadcast([P, NE, P]), ALU.is_equal)
                if t == TT - 1:
                    ins.then_inc(lo_ok, 1)

            def head_norm(s, half, chain):
                dve.wait_ge(ro_ok, 2 * s + half + 1)
                v.tensor_tensor(on[:, half, :], O[half][:, :], rstd_o[:, half, :], ALU.mult).then_inc(on_ok, 1)

            def block_step(s, last):
                chain = Chain(dve, dve_step, dve.snap(chain_reg))
                for half in range(2):
                    dve.wait_ge(t2_ok, 6 * s + 3 * half + 1)
                    v.scalar_tensor_tensor(q[:, half, :], A[0][:, :], smalls[:, 4 * DK:4 * DK + 1], t2q[:, half, :],
                                           ALU.add, ALU.mult).then_inc(qk_ok, 1)
                    for par in range(2):
                        dve.wait_ge(t2_ok, 6 * s + 3 * half + 2 + par)
                        v.scalar_tensor_tensor(kz[:, half, par, :], A[2][:, :], smalls[:, 4 * DK + 2:4 * DK + 3],
                                               t2k[:, half, par, :], ALU.add, ALU.mult).then_inc(qk_ok, 1)
                dve.wait_ge(kv_ps, s + 1)
                v.tensor_tensor(kv[:, :, :, :].rearrange("p a b m -> p (a b) m"),
                                A[3][:, :].rearrange("p (n m) -> p n m", n=4),
                                head_mask[:, :, :].rearrange("p h d -> p (h d)").unsqueeze(1).to_broadcast([P, 4, P]),
                                ALU.mult).then_inc(kv_ok, 1)
                for i in range(NGROUP):
                    dve.wait_ge(s_ps, NGROUP * s + i + 1)
                    v.tensor_tensor(s_sb[:, i % 2, :, :], S[i % 2][:, :].rearrange("p (n c) -> p n c", n=4),
                                    causal[:, :].unsqueeze(1).to_broadcast([P, 4, P]), ALU.mult).then_inc(s_ok, 1)
                    if i == 1:
                        softmax_head(s, chain)
                    if i == 2:
                        softmax_tail(s, chain)
                    if i == 3:
                        ranked_before(chain)
                    if i == 4:
                        choose(s, chain)
                    if i == 5:
                        slots(s, chain)
                    if 6 <= i < 6 + TT:
                        one_hot(s, i - 6)
                    if i == 10:
                        head_norm(s, 0, chain)
                    if i == 11 and not last:
                        norm_stats(s + 1, chain)
                    if i == 12 and not last:
                        norm_refine(s + 1, chain)
                    if i == 13 and not last:
                        norm_apply(s + 1)
                if not last:
                    front_tail(s + 1)
                dve.wait_ge(idx_ps, s + 1)
                v.tensor_tensor(idx_acc[:, :, :, :].rearrange("p e a n -> p (e a n)"),
                                A[3][:, :], idx_acc[:, :, :, :].rearrange("p e a n -> p (e a n)"),
                                ALU.add).then_inc(idx_ok, 1)
                head_norm(s, 1, chain)
                if not last:
                    logits_copy(s + 1, chain)
                dve.wait_ge(xr_in, DMA * s + DMA)
                dve.wait_ge(yout_free, DMA * s + DMA)
                for i in range(2):
                    dve.wait_ge(wo_ps, 2 * s + i + 1)
                    o = v.tensor_tensor(yout[:, 2 * i:2 * i + 2, :], O[i][:, :].rearrange("p (t d) -> p t d", t=2),
                                        xr[:, 2 * i:2 * i + 2, :], ALU.add)
                    o.then_inc(y_ok, 1)
                chain.link(v.memset(stats[:, 0, 0:1], 0.0))
                v.memset(stats[:, 0, 1:2], 0.0).then_inc(o_free, 2)
                dve.reg_add(chain_reg, chain_reg, chain.n)

            chain = Chain(dve, dve_step, None)
            norm_stats(0, chain)
            norm_refine(0, chain)
            norm_apply(0, True)
            front_tail(0)
            logits_copy(0, chain)
            dve.reg_mov(chain_reg, chain.n)
            with dve.Fori(0, NBLK - 1) as s:
                block_step(s, False)
            block_step(NBLK - 1, True)

            chain = Chain(dve, dve_step, dve.snap(chain_reg))
            dve.wait_ge(idx_ok, NBLK)
            dve.wait_ge(table_in, DMA * NBLK)
            dve.wait_ge(yout_free, DMA * (NBLK + 1))
            chain.link(v.scalar_tensor_tensor(idx_f[:, :, :], idx_acc[:, :, 1, :], float(P), idx_acc[:, :, 0, :],
                                              ALU.mult, ALU.add))
            v.tensor_copy(idx_all[:, :], idx_f[:, :, :].rearrange("p e n -> p (e n)"))
            chain.link(v.tensor_scalar(cum[0:1, 0, :], base[0:1, 0, :], float(FT - 1), None, ALU.add))
            chain.link(v.tensor_copy(cnt_i[:, :], cum[0:1, 0, :]))
            chain.link(v.tensor_scalar(cnt_i[:, :], cnt_i[:, :], FT.bit_length() - 1, None, ALU.arith_shift_right))
            chain.link(v.tensor_scalar(n_tiles[:, :], cnt_i[:, :], 1, None, ALU.max))
            v.memset(ybuf[:, :, :], 0.0).then_inc(ya_ok, 2)
            v.memset(h[:, :, 0:1], 0.0).then_inc(h_free, IC)
            v.memset(h[:, :, 1:2], 0.0).then_inc(yd_ok, 2)
            v.memset(h[:, :, 3:4], 0.0).then_inc(wt_ok, 1)
            v.memset(h[:, :, 4:5], 0.0).then_inc(tab_ok, 1)

            done = dve.alloc_register("dve_tiles")
            dve.reg_mov(done, 0)

            def tokens_lo(n):
                dve.wait_ge(ghi_ok, n + 1)
                v.tensor_tensor(gT_lo[:, :, :].rearrange("p c t -> p (c t)"), A[0][:, :],
                                gT_hi[:, :, :].rearrange("p c t -> p (c t)").bitcast(F32), ALU.subtract).then_inc(glo_ok, 1)
                v.tensor_copy(w_tok[:, bass.ds(n * (SUB * NE), SUB * NE)].rearrange("p (a e) -> p a e", a=SUB),
                              xg[:, :, D:AUG]).then_inc(wt_ok, 1)

            tokens_lo(0)
            with dve.Fori(0, NE // 2) as ep:
                for par in range(2):
                    n = dve.value_load(n_tiles[0:1, bass.ds(ep * 2 + par, 1)], min_val=1, max_val=MAX_TILES)
                    with dve.Fori(0, n):
                        t = dve.snap(done, min_val=0, max_val=NE * MAX_TILES - 1)
                        for ic in range(IC):
                            dve.wait_ge(silu_ok, t * IC + (ic + 1))
                            v.tensor_tensor(h[:, ic, :], sg[:, ic, :], bank_gu(ic)[:, FT:2 * FT], ALU.mult).then_inc(h_free, 1)
                            dve.wait_ge(hhi_ok, t * IC + (ic + 1))
                            v.tensor_tensor(h_lo[:, ic, :], h[:, ic, :], h_hi[:, ic, :].bitcast(F32),
                                            ALU.subtract).then_inc(hlo_ok, 1)
                        tokens_lo(t + 1)
                        dve.wait_ge(y_ps, t * SUB + 2)
                        dve.wait_ge(scattered, (t + 3) * (SUB * DMA))
                        v.tensor_scalar(ybuf[:, 1, :], O[1][:, 0:D],
                                        w_tok[:, bass.ds(t * (SUB * NE) + (NE + par) + ep * 2, 1)], None,
                                        ALU.mult).then_inc(yd_ok, 1)
                        dve.reg_add(done, done, 1)

        @block.tensor
        def _(pe):
            mm = nc.tensor.matmul

            def product(out_ap, l_hi, l_lo, r_hi, r_lo, n, k):
                mm(out_ap, l_hi, r_hi, start=(k == 0), stop=False)
                mm(out_ap, l_hi, r_lo, start=False, stop=False)
                return mm(out_ap, l_lo, r_hi, start=False, stop=(k == n - 1))

            pe.wait_ge(natural, DMA)
            for f in range(4):
                pe.wait_ge(feat_ok, f + 1)
                for kc in range(KC):
                    for hc in range(2):
                        last = mm(A[f][:, kc * D + hc * P:kc * D + hc * P + P], nat[:, f // 2, hc, kc * P:(kc + 1) * P],
                                  feat[:, f, :], start=True, stop=True)
                last.then_inc(fused_ps, 1)
            pe.wait_ge(fused_ps, 4)
            pe.nop().then_inc(split_ok, 1)
            pe.wait_ge(fused_ok, 4)

            def transposes(s, first=False):
                pe.wait_ge(xn_ok, s + 1)
                if not first:
                    pe.wait_ge(on_ok, 2 * s - 1)
                for c in range(KC):
                    for t in range(TT):
                        last = nc.tensor.transpose(A[c][:, t * P:(t + 1) * P], xna[:, t, c * P:(c + 1) * P], ident[:, :])
                    last.then_inc(xt_ps, 1)

            def logits(s, first=False):
                pe.wait_ge(xlo_ok, KC * s + KC)
                if not first:
                    pe.wait_ge(idx_ok, s)
                for t in range(TT):
                    for c in range(KC):
                        tok = slice(t * P, (t + 1) * P)
                        last = product(A[3][:, t * NE:(t + 1) * NE], xT_hi[:, c, tok], xT_lo[:, c, tok],
                                       rt_hi[:, c, :], rt_lo[:, c, :], KC, c)
                last.then_inc(lg_ps, 1)

            def project(bank, f, half):
                w = slice(half * P, (half + 1) * P)
                for c in range(KC):
                    last = product(bank[:, :], wqk_hi[:, f, c, w], wqk_lo[:, f, c, w], xT_hi[:, c, :], xT_lo[:, c, :], KC, c)
                return last

            def scores(s, i):
                half, b, g = i // 8, i // 4 % 2, i % 4
                if i % 8 == 0:
                    pe.wait_ge(qk_ok, 6 * s + 3 * half + 3)
                rows = slice(32 * g, 32 * g + 32)
                for t in range(2):
                    tok = slice((2 * b + t) * P, (2 * b + t + 1) * P)
                    for par in range(2):
                        n = 2 * t + par
                        last = mm(S[i % 2][:, n * P:(n + 1) * P], kz[rows, half, par, tok], q[rows, half, tok],
                                  start=True, stop=True, tile_position=(32 * g, 0))
                last.then_inc(s_ps, 1)

            def values(s, i):
                half, b, g = i // 8, i // 4 % 2, i % 4
                if i == 0:
                    pe.wait_ge(v_ok, 2 * s + 2)
                    pe.wait_ge(kv_ok, s + 1)
                    pe.wait_ge(o_free, 2 * s + 2)
                if i % 4 == 0:
                    tok = slice((2 * b + 1) * P, (2 * b + 2) * P)
                    mm(O[half][:, tok], kv[:, half, b, :], q[:, half, tok], start=True, stop=True, skip_group_check=True)
                pe.wait_ge(s_ok, NGROUP * s + i + 1)
                for t in range(2):
                    tok = slice((2 * b + t) * P, (2 * b + t + 1) * P)
                    for par in range(2):
                        w = vz[:, 2 * b + t, half * PAIRS + g, 2 * par:2 * par + 2, :].rearrange("p a d -> p (a d)")
                        last = mm(O[half][32 * g:32 * g + 32, tok], w, s_sb[:, i % 2, 2 * t + par, :],
                                  start=False, stop=True, skip_group_check=True, tile_position=(0, 32 * g))
                last.then_inc(pv_ps, 1)

            def mean_squares(s, half):
                pe.wait_ge(sq_ok, 2 * s + half + 1)
                if half == 1:
                    pe.wait_ge(rank_ok, s + 1)
                mm((A[0] if half == 0 else A[2])[:, :], head_mean[:, :], sq[:, half, :], start=True,
                   stop=True).then_inc(ms_ps, 1)

            def block_step(s, last):
                pe.wait_ge(lg_ok, s + 1)
                for half in range(2):
                    if half == 1:
                        pe.wait_ge(qk_ok, 6 * s + 1)
                    project(A[0], 0, half)
                    project(A[1], 1, half).then_inc(proj_ps, 1)
                    if half == 1:
                        pe.wait_ge(qk_ok, 6 * s + 3)
                    project(A[2], 2, half)
                    project(A[3], 3, half).then_inc(proj_ps, 1)
                pe.wait_ge(qk_ok, 6 * s + 4)
                for t in range(TT):
                    tok = slice(t * P, (t + 1) * P)
                    for c in range(KC):
                        o = product(A[t // 2][:, t % 2 * D:(t % 2 + 1) * D], xT_hi[:, c, tok], xT_lo[:, c, tok],
                                    wvo_hi[:, 0, c, :], wvo_lo[:, 0, c, :], KC, c)
                    if t % 2:
                        o.then_inc(proj_ps, 1)
                pe.wait_ge(kf_ok, 2 * s + 2)
                pe.wait_ge(qk_ok, 6 * s + 6)
                for half in range(2):
                    for b in range(2):
                        o = nc.tensor.transpose(A[2][:, (2 * half + b) * P:(2 * half + b + 1) * P], kf[:, half, b, :],
                                                ident[:, :])
                o.then_inc(kt_ps, 1)
                scores(s, 0)
                scores(s, 1)
                pe.wait_ge(kt_ok, s + 1)
                pe.wait_ge(v_ok, 2 * s + 2)
                for half in range(2):
                    for b in range(2):
                        rhs = vz[:, 2 * b, half * PAIRS:(half + 1) * PAIRS, 0:4:3, :]
                        o = mm(A[3][:, (2 * half + b) * P:(2 * half + b + 1) * P], k_tok[:, half, b, :], rhs,
                               start=True, stop=True)
                o.then_inc(kv_ps, 1)
                for i in range(NGROUP):
                    values(s, i)
                    if i + 2 < NGROUP:
                        scores(s, i + 2)
                    if i == 5:
                        pe.wait_ge(sel_ok, s + 1)
                        chosen = sel[:, :, :].rearrange("p t e -> p (t e)")
                        mm(A[2][:, 0:TT * NE], before[:, :], chosen, start=True, stop=True)
                        mm(A[2][:, TT * NE:2 * TT * NE], ones_bf[:, :], chosen, start=True, stop=True).then_inc(rank_ps, 1)
                    if i == 8:
                        mean_squares(s, 0)
                if not last:
                    transposes(s + 1)
                pe.wait_ge(oh_ok, s + 1)
                pe.wait_ge(lo_ok, s + 1)
                for e in range(NE):
                    for t in range(TT):
                        n = t * NE + e
                        o = mm(A[3][:, e * 64:(e + 1) * 64], oh_lo[:, n, :],
                               oh_rhs[:, n, :, :].rearrange("p a n -> p (a n)"), start=(t == 0), stop=(t == TT - 1))
                o.then_inc(idx_ps, 1)
                mean_squares(s, 1)
                if not last:
                    logits(s + 1)
                pe.wait_ge(onlo_ok, 2 * s + 2)
                for t in range(TT):
                    tok = slice(t * P, (t + 1) * P)
                    for half in range(2):
                        o = product(O[t // 2][:, t % 2 * D:(t % 2 + 1) * D], on_hi[:, half, tok], on_lo[:, half, tok],
                                    wvo_hi[:, 1, half, :], wvo_lo[:, 1, half, :], 2, half)
                    if t % 2:
                        o.then_inc(wo_ps, 1)

            transposes(0, True)
            logits(0, True)
            with pe.Fori(0, NBLK - 1) as s:
                block_step(s, False)
            block_step(NBLK - 1, True)

            pe.nop().then_inc(xg_free, 1)
            pe.nop().then_inc(w_free, 1)
            pe.wait_ge(tab_ok, 1)
            pe.wait_ge(o_free, 2 * NBLK + 2)
            done = pe.alloc_register("pe_tiles")
            pe.reg_mov(done, 0)

            def tokens(n):
                pe.wait_ge(gathered, n * (SUB * DMA) + SUB * DMA)
                for c in range(KC):
                    for sub in range(SUB):
                        last = nc.tensor.transpose(A[0][:, c * FT + sub * P:c * FT + (sub + 1) * P],
                                                   xg[:, sub, c * P:(c + 1) * P], ident[:, :])
                last.then_inc(xg_free, 1)

            tokens(0)
            pe.nop()
            with pe.Fori(0, NE // 2) as ep:
                for par in range(2):
                    n = pe.value_load(n_tiles[0:1, bass.ds(ep * 2 + par, 1)], min_val=1, max_val=MAX_TILES)
                    pe.wait_ge(wsplit, ep * (2 * PIECES) + PIECES * (par + 1))
                    pe.sem_inc(pe_gate, 1)
                    with pe.Fori(0, n):
                        t = pe.snap(done)
                        pe.wait_ge(glo_ok, t + 1)
                        for ic in range(IC):
                            pe.wait_ge(h_free, t * IC + (ic + 1))
                            for m in range(2):
                                for c in range(KC):
                                    w = slice(m * KC * NI + c * NI + ic * P, m * KC * NI + c * NI + (ic + 1) * P)
                                    last = product(bank_gu(ic)[:, m * FT:(m + 1) * FT], w_hi[par][:, w], w_lo[par][:, w],
                                                   gT_hi[:, c, :], gT_lo[:, c, :], KC, c)
                            last.then_inc(gu_ps, 1)
                        tokens(t + 1)
                        pe.wait_ge(ya_ok, t + 2)
                        pe.wait_ge(yd_ok, t + 2)
                        for ic in range(IC):
                            pe.wait_ge(hlo_ok, t * IC + (ic + 1))
                            w = slice(down0 + ic * D, down0 + (ic + 1) * D)
                            for sub in range(SUB):
                                tok = slice(sub * P, (sub + 1) * P)
                                last = product(O[sub][:, 0:D], h_hi[:, ic, tok], h_lo[:, ic, tok],
                                               w_hi[par][:, w], w_lo[par][:, w], IC, ic)
                                if ic == IC - 1:
                                    last.then_inc(y_ps, 1)
                        pe.reg_add(done, done, 1)
                    pe.wait_ge(y_ps, pe.snap(done) * SUB)
                    pe.nop().then_inc(w_free, 1)


def kernel(**inputs):
    import numpy as np
    import concourse.bacc as bacc
    from concourse.bass_utils import run_bass_kernel_spmd

    a = {n.replace("L0_attn_", "").replace("L0_ffn_", ""): np.asarray(v) for n, v in inputs.items()}
    by_row = lambda w: w.reshape(KC, P, -1).transpose(1, 0, 2)
    heads = lambda v: np.tile(v, (HH, 1))
    arrays = {
        "x": a["x"].reshape(NT, D),
        "wqk_nat": np.stack([by_row(a["wq"]), by_row(a["wk"])], 1),
        "small": np.concatenate([heads(a[n].T) for n in ("fq1_w", "fq2_w", "fk1_w", "fk2_w")]
                                + [heads(a[n][:, None]) for n in ("fq1_b", "fq2_b", "fk1_b", "fk2_b", "norm_w")], 1),
        "wvo": np.stack([by_row(a["wv"].T), by_row(a["wo"].T)], 1),
        "router": by_row(a["router_w"].T),
        "wffn": np.concatenate([
            w.transpose(0, 2, 1).reshape(NE, -1, P, w.shape[1]).transpose(0, 2, 1, 3).reshape(NE, P, -1)
            for w in (a["gate_w"], a["up_w"], a["down_w"])], 2),
    }
    arrays = {n: np.ascontiguousarray(v) for n, v in arrays.items()}
    nc = bacc.Bacc("TRN2", target_bir_lowering=False, num_devices=1)
    args = {n: nc.dram_tensor(n, v.shape, mybir.dt.from_np(v.dtype), kind="ExternalInput").ap()
            for n, v in arrays.items()}
    out = nc.dram_tensor("out", [NT, D], F32, kind="ExternalOutput").ap()
    build(nc, out=out, **args)
    r = run_bass_kernel_spmd(nc, [arrays], core_ids=[0])
    return r.results[0]["out"].reshape(inputs["L0_attn_x"].shape)
```

```python
from contextlib import ExitStack

import concourse.bass as bass
from concourse import mybir
from concourse.alu_op_type import AluOpType as ALU

F32 = mybir.dt.float32
F32R = mybir.dt.float32r
BF16 = mybir.dt.bfloat16
I32 = mybir.dt.int32
U32 = mybir.dt.uint32
ACT = mybir.ActivationFunctionType
X_AXIS = mybir.AxisListType.X

P = 128
NT = 4096
D = 256
KC = D // P
BLK = 512
NBLK = NT // BLK
TT = BLK // P
DK = 16
HH = P // DK
PAIRS = HH // 2
NE = 8
NI = 512
IC = NI // P
TOP_P = 0.9
LN_EPS = 1e-5
RMS_EPS = 1e-5
AUG = D + NE
FT = 256
SUB = FT // P
MAX_TILES = NT // FT
WE = KC * NI * 2 + IC * D
PIECES = 4
PW = WE // PIECES
NGROUP = 2 * 2 * PAIRS
NS = 4
DMA = 16


class Chain:

    def __init__(self, eng, sem, base=None):
        self.eng, self.sem, self.base, self.n = eng, sem, base, 0

    def link(self, ins):
        ins.then_inc(self.sem, 1)
        self.n += 1
        self.eng.wait_ge(self.sem, self.n if self.base is None else self.base + self.n)


def build(nc, x, wqk_nat, small, wvr, wo, wffn, out):
    ctx = ExitStack()
    with ctx:
        def sb(name, shape, dt=F32):
            return ctx.enter_context(nc.sbuf_tensor(name, shape, dt))

        def ps(name, shape, dt=F32):
            return ctx.enter_context(nc.psum_tensor(name, shape, dt))

        def sem(name):
            return ctx.enter_context(nc.semaphore(name))

        x_blk = x.rearrange("(s t p) d -> s p t d", t=TT, p=P)
        out_blk = out.rearrange("(s t p) d -> s p t d", t=TT, p=P)
        table = nc.dram_tensor("gather_table", [NT, AUG], F32, kind="Internal").ap()
        table_blk = table.rearrange("(s t p) d -> s p t d", t=TT, p=P)

        ident = sb("ident", [P, P])
        head_mask = sb("head_mask", [P, HH, DK])
        head_mean = sb("head_mean", [P, P])
        causal = sb("causal", [P, P])
        before = sb("before", [P, P], BF16)
        ones_bf = sb("ones_bf", [P, P], BF16)
        lo_iota = sb("lo_iota", [P, P])
        hi_iota = sb("hi_iota", [P, NT // P])
        part = sb("part", [P, 1])
        lower_e = sb("lower_e", [P, NE, NE])
        parity = sb("parity", [P, 2])
        parity_b = sb("parity_b", [P, 2])
        eps = sb("eps", [P, 1])
        bq2 = sb("bq2", [P, 1])
        smalls = sb("smalls", [P, 4 * DK + 5])
        wqk_hi = sb("wqk_hi", [P, 4, KC, D], F32R)
        wqk_lo = sb("wqk_lo", [P, 4, KC, D], F32R)
        wvr_hi = sb("wvr_hi", [P, KC, AUG], F32R)
        wvr_lo = sb("wvr_lo", [P, KC, AUG], F32R)
        wo_hi = sb("wo_hi", [P, KC, D], F32R)
        wo_lo = sb("wo_lo", [P, KC, D], F32R)
        feat = sb("feat", [P, 4, P])
        w_raw = sb("w_raw", [P, WE])
        w_hi = [sb(f"w_hi{i}", [P, WE], F32R) for i in range(2)]
        w_lo = [sb(f"w_lo{i}", [P, WE], F32R) for i in range(2)]
        base = sb("base", [P, TT + 1, NE])
        from_end = sb("from_end", [P, TT])
        tile_no = sb("tile_no", [P, TT])
        idx_acc = sb("idx_acc", [P, NE, 2, NT // P])
        idx_all = sb("idx_all", [P, NE * (NT // P)], U32)
        n_tiles = sb("n_tiles", [1, NE], I32)

        ph1 = ExitStack()

        def sb1(name, shape, dt=F32):
            return ph1.enter_context(nc.sbuf_tensor(name, shape, dt))

        xa = sb1("xa", [P, TT, D])
        stats = sb1("stats", [P, TT, 6])
        mv = sb1("mv", [P, TT, 2])
        rstd_x = sb1("rstd_x", [P, TT])
        var_eps = sb1("var_eps", [P, TT])
        newton = sb1("newton", [P, TT])
        ln_x = sb1("ln_x", [P, TT])
        ln_o = sb1("ln_o", [P, 2, BLK])
        slot_i = sb1("slot_i", [P, TT, NE], I32)
        lo_i = sb1("lo_i", [P, TT, NE], I32)
        xna = sb1("xna", [P, TT, AUG])
        xT_hi = sb1("xT_hi", [P, KC, BLK], F32R)
        xT_lo = sb1("xT_lo", [P, KC, BLK], F32R)
        t2q = sb1("t2q", [P, 2, BLK])
        t2k = sb1("t2k", [P, 2, 2, BLK])
        q = sb1("q", [P, 2, BLK])
        kz = sb1("kz", [P, 2, 2, BLK])
        kf = sb1("kf", [P, 2, 2, P])
        k_tok = sb1("k_tok", [P, 2, 2, P])
        kv = sb1("kv", [P, 2, 2, P])
        vz = sb1("vz", [P, TT, 2 * PAIRS, 4, DK])
        s_sb = sb1("s_sb", [P, NS, 4, P])
        sq = sb1("sq", [P, 2, BLK])
        rstd_o = sb1("rstd_o", [P, 2, BLK])
        on = sb1("on", [P, 2, BLK])
        on_hi = sb1("on_hi", [P, 2, BLK], F32R)
        on_lo = sb1("on_lo", [P, 2, BLK], F32R)
        xr = sb1("xr", [P, TT, D])
        yout = sb1("yout", [P, TT, D])
        lg = sb1("lg", [P, TT, NE])
        mx = sb1("mx", [P, TT])
        ls = sb1("ls", [P, TT, NE])
        ex = sb1("ex", [P, TT, NE])
        sm = sb1("sm", [P, TT])
        pr = sb1("pr", [P, TT, NE])
        c_gt = sb1("c_gt", [P, TT, NE, NE])
        c_eq = sb1("c_eq", [P, TT, NE, NE])
        cum = sb1("cum", [P, TT, NE])
        keep = sb1("keep", [P, TT, NE])
        sel = sb1("sel", [P, TT, NE], BF16)
        slot = sb1("slot", [P, TT, NE])
        slot_lo = sb1("slot_lo", [P, TT, NE])
        slot_hi = sb1("slot_hi", [P, TT, NE])
        oh_lo = sb1("oh_lo", [P, TT * NE, P], BF16)
        oh_hi = sb1("oh_hi", [P, TT * NE, NT // P])
        oh_rhs = sb1("oh_rhs", [P, TT * NE, 2, NT // P], BF16)
        ph1.close()

        ph2 = ctx.enter_context(ExitStack())

        def sb2(name, shape, dt=F32):
            return ph2.enter_context(nc.sbuf_tensor(name, shape, dt))

        idx_f = sb2("idx_f", [P, NE, NT // P])
        cnt_i = sb2("cnt_i", [1, NE], I32)
        xg = sb2("xg", [P, SUB, AUG])
        g_idx = sb2("g_idx", [P, SUB], U32)
        s_idx = sb2("s_idx", [P, SUB], U32)
        gT_hi = sb2("gT_hi", [P, KC, FT], F32R)
        gT_lo = sb2("gT_lo", [P, KC, FT], F32R)
        sg = sb2("sg", [P, IC, FT])
        h = sb2("h", [P, IC, FT])
        h_hi = sb2("h_hi", [P, IC, FT], F32R)
        h_lo = sb2("h_lo", [P, IC, FT], F32R)
        ybuf = sb2("ybuf", [P, SUB, D])
        w_tok = sb2("w_tok", [P, (NE * MAX_TILES + 1) * SUB * NE])

        A_all = ps("A_all", [P, 4, 512])
        A = [A_all[:, i, :] for i in range(4)]
        S = [ps(f"S{i}", [P, 512]) for i in range(2)]
        scores_banks = S + A[0:2]
        values_banks = [A[2], A[3], A[0], A[1]]
        O = [ps(f"O{i}", [P, 512]) for i in range(2)]

        names = ("loads natural masks feat_ok fused_ps fused_ok split_ok setup_dve setup_act "
                 "x_in xn_ok xt_ps xhi_ok xlo_ok lg_ok proj_ps t2_ok qk_ok v_ps v_ok kf_ok kt_ps kt_ok kv_ps kv_ok "
                 "s_ps s_ok pv_ps sq_ok ms_ps ro_ok var_ok rs0_ok ln_x_ok ln_o_ok on_ok onhi_ok onlo_ok wo_ps o_free xr_in yout_free y_ok "
                 "ls_ok ex_ok sel_ok rank_ps rank_ok slot_ok lo_ok oh_ok idx_ps idx_ok w_ok table_in "
                 "dve_step pool_step act_step tab_ok w_in wsplit w_free "
                 "gi_step gathered xg_free ghi_ok glo_ok gu_ps silu_ok h_free hhi_ok hlo_ok y_ps ya_ok yd_ok "
                 "wt_ok scattered pool_gate dve_gate pe_gate")
        sems = {n: sem(n) for n in names.split()}
        (loads, natural, masks, feat_ok, fused_ps, fused_ok, split_ok, setup_dve, setup_act,
         x_in, xn_ok, xt_ps, xhi_ok, xlo_ok, lg_ok, proj_ps, t2_ok, qk_ok, v_ps, v_ok, kf_ok, kt_ps, kt_ok, kv_ps, kv_ok,
         s_ps, s_ok, pv_ps, sq_ok, ms_ps, ro_ok, var_ok, rs0_ok, ln_x_ok, ln_o_ok, on_ok, onhi_ok, onlo_ok, wo_ps, o_free, xr_in, yout_free, y_ok,
         ls_ok, ex_ok, sel_ok, rank_ps, rank_ok, slot_ok, lo_ok, oh_ok, idx_ps, idx_ok, w_ok, table_in,
         dve_step, pool_step, act_step, tab_ok, w_in, wsplit, w_free,
         gi_step, gathered, xg_free, ghi_ok, glo_ok, gu_ps, silu_ok, h_free, hhi_ok, hlo_ok, y_ps, ya_ok, yd_ok,
         wt_ok, scattered, pool_gate, dve_gate, pe_gate) = [sems[n] for n in names.split()]

        nat = w_raw[:, 0:2 * KC * D].rearrange("p (m c k) -> p m c k", m=2, c=KC)
        wvr_raw = w_raw[:, 2 * KC * D:2 * KC * D + KC * AUG].rearrange("p (c k) -> p c k", c=KC)
        wo_raw = w_raw[:, 2 * KC * D + KC * AUG:3 * KC * D + KC * AUG].rearrange("p (c k) -> p c k", c=KC)
        down0 = 2 * KC * NI

        def bank_gu(ic):
            return (A[1], A[2], A[3], S[0])[ic]

        block = ctx.enter_context(nc.Block())

        @block.sync
        def _(sp):
            sp.dma_start(xa[:, :, :], x_blk[0]).then_inc(x_in, DMA)
            sp.dma_start(smalls[:, :], small).then_inc(loads, DMA)
            sp.dma_start(nat, wqk_nat).then_inc(natural, DMA)
            sp.dma_start(wvr_raw, wvr).then_inc(loads, DMA)
            sp.dma_start(wo_raw, wo).then_inc(loads, DMA)
            sp.wait_ge(split_ok, 2)
            sp.dma_start(w_raw[:, :], wffn[0]).then_inc(w_in, DMA)

            def block_step(s, last):
                if not last:
                    sp.wait_ge(xn_ok, s + 1)
                    sp.dma_start(xa[:, :, :], x_blk[s + 1]).then_inc(x_in, DMA)
                sp.wait_ge(o_free, 2 * s + 2)
                sp.dma_start(xr[:, :, :], x_blk[s]).then_inc(xr_in, DMA)
                sp.wait_ge(w_ok, s + 1)
                sp.dma_start(table_blk[s], xna[:, :, :]).then_inc(table_in, DMA)
                sp.wait_ge(y_ok, 2 * s + 2)
                sp.dma_start(out_blk[s], yout[:, :, :]).then_inc(yout_free, DMA)

            with sp.Fori(0, NBLK - 1) as s:
                block_step(s, False)
            block_step(NBLK - 1, True)
            for e in range(1, NE):
                sp.wait_ge(wsplit, PIECES * e)
                sp.dma_start(w_raw[:, :], wffn[e]).then_inc(w_in, DMA)

        @block.gpsimd
        def _(pool):
            g = nc.gpsimd
            g.memset(ident[:, :], 0.0).then_inc(pool_step, 1)
            g.memset(head_mask[:, :, :], 1.0).then_inc(pool_step, 1)
            g.memset(causal[:, :], 1.0).then_inc(pool_step, 1)
            g.memset(before[:, :], 1.0).then_inc(pool_step, 1)
            g.memset(lower_e[:, :, :], 1.0).then_inc(pool_step, 1)
            pool.wait_ge(pool_step, 5)
            g.affine_select(out=ident[:, :], in_=ident[:, :], compare_op=ALU.not_equal, fill=1.0,
                            base=0, pattern=[[-1, P]], channel_multiplier=1).then_inc(pool_step, 1)
            g.affine_select(out=head_mask[:, :, :], in_=head_mask[:, :, :], compare_op=ALU.is_ge, fill=0.0,
                            base=0, pattern=[[-DK, HH], [0, DK]], channel_multiplier=1).then_inc(pool_step, 1)
            g.affine_select(out=causal[:, :], in_=causal[:, :], compare_op=ALU.is_ge, fill=0.0,
                            base=0, pattern=[[1, P]], channel_multiplier=-1).then_inc(pool_step, 1)
            g.affine_select(out=before[:, :], in_=before[:, :], compare_op=ALU.is_ge, fill=0.0,
                            base=-1, pattern=[[1, P]], channel_multiplier=-1).then_inc(pool_step, 1)
            g.affine_select(out=lower_e[:, :, :], in_=lower_e[:, :, :], compare_op=ALU.is_ge, fill=0.0,
                            base=-1, pattern=[[1, NE], [-1, NE]], channel_multiplier=0).then_inc(pool_step, 1)
            pool.wait_ge(pool_step, 10)
            g.affine_select(out=head_mask[:, :, :], in_=head_mask[:, :, :], compare_op=ALU.is_ge, fill=0.0,
                            base=DK - 1, pattern=[[DK, HH], [0, DK]], channel_multiplier=-1).then_inc(pool_step, 1)
            pool.wait_ge(pool_step, 11)
            g.memset(ones_bf[:, :], 1.0)
            g.memset(eps[:, :], RMS_EPS)
            g.iota(lo_iota[:, :], pattern=[[1, P]], base=0, channel_multiplier=0, allow_small_or_imprecise_dtypes=True)
            g.iota(hi_iota[:, :], pattern=[[P, NT // P]], base=0, channel_multiplier=0,
                   allow_small_or_imprecise_dtypes=True)
            g.iota(part[:, :], pattern=[[0, 1]], base=0, channel_multiplier=1, allow_small_or_imprecise_dtypes=True)
            g.iota(from_end[:, :], pattern=[[-P, TT]], base=NT - 1, channel_multiplier=-1,
                   allow_small_or_imprecise_dtypes=True)
            g.iota(tile_no[:, :], pattern=[[1, TT]], base=0, channel_multiplier=0,
                   allow_small_or_imprecise_dtypes=True)
            g.memset(base[:, :, :], 0.0)
            g.memset(idx_acc[:, :, :, :], 0.0)
            g.memset(vz[:, :, :, :, :], 0.0)
            g.memset(yout[:, :, :], 0.0).then_inc(yout_free, DMA)
            g.tensor_scalar(head_mean[:, :], head_mask[:, :, :].rearrange("p h d -> p (h d)"), 1.0 / DK, None,
                            ALU.mult).then_inc(masks, 1)
            b_reg = pool.alloc_register("pool_base")
            pool.reg_mov(b_reg, 11)

            def first_keys(s):
                for half in range(2):
                    pool.wait_ge(qk_ok, 6 * s + 3 * half + 3)
                    first = [kz[:, half, par, :].rearrange("p (b c m) -> p b c m", b=2, c=2)[:, :, 0, :]
                             for par in range(2)]
                    g.tensor_tensor(kf[:, half, :, :], first[0], first[1], ALU.add).then_inc(kf_ok, 1)

            def block_step(s, last):
                chain = Chain(pool, pool_step, pool.snap(b_reg))
                pool.wait_ge(slot_ok, s + 1)
                pool.sem_inc(pool_gate, 1)
                g.tensor_scalar(oh_rhs[:, :, 0, :], oh_hi[:, :, :], part[:, 0:1], None, ALU.mult)
                for t in range(TT):
                    one_hots = g.tensor_scalar(oh_rhs[:, t * NE:(t + 1) * NE, 1, :], oh_hi[:, t * NE:(t + 1) * NE, :],
                                           tile_no[:, t:t + 1], None, ALU.mult)
                one_hots.then_inc(oh_ok, 1)
                pool.wait_ge(oh_ok, s + 1)
                pool.sem_inc(pool_gate, 1)
                chain.link(g.tensor_scalar(tile_no[:, :], tile_no[:, :], float(TT), None, ALU.add))
                for half in range(2):
                    pool.wait_ge(onhi_ok, 2 * s + half + 1)
                    g.tensor_tensor(on_lo[:, half, :], on[:, half, :], on_hi[:, half, :].bitcast(F32),
                                    ALU.subtract).then_inc(onlo_ok, 1)
                if not last:
                    first_keys(s + 1)
                pool.reg_add(b_reg, b_reg, chain.n)

            first_keys(0)
            with pool.Fori(0, NBLK - 1) as s:
                block_step(s, False)
            block_step(NBLK - 1, True)

            def split_piece(par, c0):
                raw = w_raw[:, bass.ds(c0, PW)]
                whi = w_hi[par][:, bass.ds(c0, PW)]
                wlo = w_lo[par][:, bass.ds(c0, PW)]
                link(g.tensor_copy(whi, raw))
                g.tensor_tensor(wlo, raw, whi.bitcast(F32), ALU.subtract).then_inc(wsplit, 1)

            step = pool.alloc_register("pool_steps")
            pool.reg_mov(step, b_reg)

            def link(ins):
                ins.then_inc(pool_step, 1)
                pool.wait_ge(pool_step, pool.snap(step) + 1)
                pool.reg_add(step, step, 1)
                pool.sem_inc(pool_gate, 1)

            pool.wait_ge(w_in, DMA)
            for piece in range(PIECES):
                split_piece(0, piece * PW)
            pool.wait_ge(tab_ok, 1)
            pool.wait_ge(table_in, DMA * NBLK)
            pool.wait_ge(yout_free, DMA * (NBLK + 1))

            done = pool.alloc_register("tiles_done")
            col1 = pool.alloc_register("col1")
            col2 = pool.alloc_register("col2")
            pieces = pool.alloc_register("pieces")
            piece_col = pool.alloc_register("piece_col")
            for r in (done, col1, col2):
                pool.reg_mov(r, 0)

            def gather(col):
                n = pool.snap(done)
                pool.wait_ge(xg_free, n + 1)
                pool.wait_ge(wt_ok, n + 1)
                pool.sem_inc(pool_gate, 1)
                link(g.tensor_copy(g_idx[:, :], idx_all[:, bass.ds(col, SUB)]))
                for sub in range(SUB):
                    pool.indirect_dma_start(
                        out=xg[:, sub, :], out_offset=None, in_=table,
                        in_offset=bass.IndirectOffsetOnAxis(ap=g_idx[:, sub:sub + 1], axis=0)).then_inc(gathered, DMA)

            def scatter():
                n = pool.snap(done)
                pool.wait_ge(ya_ok, n + 1)
                pool.wait_ge(yd_ok, n + 1)
                pool.wait_ge(scattered, (n + 1) * (SUB * DMA))
                pool.sem_inc(pool_gate, 1)
                link(g.tensor_copy(s_idx[:, :], idx_all[:, bass.ds(pool.snap(col2, min_val=0, max_val=NE * (NT // P) - SUB), SUB)]))
                add_rows()
                pool.reg_add(done, done, 1)

            def add_rows():
                for sub in range(SUB):
                    pool.indirect_dma_start(
                        out=out, out_offset=bass.IndirectOffsetOnAxis(ap=s_idx[:, sub:sub + 1], axis=0),
                        in_=ybuf[:, sub, :], in_offset=None, compute_op=ALU.add).then_inc(scattered, DMA)

            pool.wait_ge(ya_ok, 2)
            link(g.tensor_copy(s_idx[:, :], idx_all[:, 0:SUB]))
            add_rows()

            with pool.Fori(0, NE // 2) as ep:
                for par in range(2):
                    pool.reg_mov(pieces, PIECES)
                    if par == 1:
                        with pool.If(ep > NE // 2 - 2):
                            pool.reg_mov(pieces, 0)
                        pool.sem_inc(pool_gate, 1)
                    n = pool.value_load(n_tiles[0:1, bass.ds(ep * 2 + par, 1)], min_val=1, max_val=MAX_TILES)
                    with pool.Fori(0, n) as j:
                        col = pool.snap(ep * (2 * NT // P) + (par * (NT // P)) + j * SUB)
                        gather(col)
                        scatter()
                        pool.reg_mov(col2, col1)
                        pool.reg_mov(col1, col)
                        with pool.If(j < pool.snap(pieces)):
                            pool.wait_ge(w_free, ep * 2 + (par + 1))
                            pool.wait_ge(w_in, (ep * 2 + (par + 2)) * DMA)
                            pool.sem_inc(pool_gate, 1)
                            pool.reg_mov(piece_col, j * PW)
                            split_piece(1 - par, pool.snap(piece_col, min_val=0, max_val=(PIECES - 1) * PW))
                        pool.sem_inc(pool_gate, 1)
                    for piece in range(1, PIECES):
                        with pool.If(n + PIECES - pool.snap(pieces) < piece + 1):
                            pool.wait_ge(w_free, ep * 2 + (par + 1))
                            pool.wait_ge(w_in, (ep * 2 + (par + 2)) * DMA)
                            pool.sem_inc(pool_gate, 1)
                            split_piece(1 - par, piece * PW)
                        pool.sem_inc(pool_gate, 1)
            gather(0)
            scatter()
            pool.reg_mov(col2, col1)
            scatter()
            pool.wait_ge(scattered, (pool.snap(done) + 1) * (SUB * DMA))

        @block.scalar
        def _(act):
            a = nc.scalar
            for f in range(4):
                act.wait_ge(fused_ps, f + 1)
                a.activation(wqk_hi[:, f, :, :].rearrange("p c n -> p (c n)"), A[f][:, :], ACT.Copy).then_inc(setup_act, 1)

            def token_rstd(s):
                act.wait_ge(var_ok, s + 1)
                a.activation(ln_x[:, :], var_eps[:, :], ACT.Ln).then_inc(ln_x_ok, 1)
                act.wait_ge(ln_x_ok, s + 1)
                a.activation(rstd_x[:, :], ln_x[:, :], ACT.Exp, scale=-0.5).then_inc(rs0_ok, 1)

            def head_rstd(s, half):
                act.wait_ge(ms_ps, 2 * s + half + 1)
                a.activation(ln_o[:, half, :], A[3 - half][:, :], ACT.Ln, bias=eps[:, 0:1]).then_inc(ln_o_ok, 1)
                act.wait_ge(ln_o_ok, 2 * s + half + 1)
                a.activation(rstd_o[:, half, :], ln_o[:, half, :], ACT.Exp, scale=-0.5).then_inc(ro_ok, 1)

            def heads_hi(s, half):
                act.wait_ge(on_ok, 2 * s + half + 1)
                a.activation(on_hi[:, half, :], on[:, half, :], ACT.Copy).then_inc(onhi_ok, 1)

            def front(s):
                for c in range(KC):
                    act.wait_ge(xt_ps, KC * s + c + 1)
                    a.activation(xT_hi[:, c, :], S[c][:, :], ACT.Copy).then_inc(xhi_ok, 1)

            def second_maps(s):
                for half in range(2):
                    act.wait_ge(proj_ps, 4 * s + 2 * half + 1)
                    a.activation(t2q[:, half, :], A[1][:, :], ACT.Identity, bias=bq2[:, 0:1],
                                 scale=DK ** -0.5).then_inc(t2_ok, 1)
                    act.wait_ge(proj_ps, 4 * s + 2 * half + 2)
                    for par in range(2):
                        a.activation(t2k[:, half, par, :], A[3][:, :], ACT.Identity, bias=parity_b[:, par:par + 1],
                                     scale=parity[:, par:par + 1]).then_inc(t2_ok, 1)

            def block_step(s, last):
                for t in range(TT):
                    act.wait_ge(v_ps, TT * s + t + 1)
                    a.activation(vz[:, t, :, 0:4:3, :], values_banks[t][:, 0:D].rearrange("p (g e d) -> p g e d", e=2, d=DK),
                                 ACT.Copy).then_inc(v_ok, 1)
                act.wait_ge(kt_ps, s + 1)
                a.activation(k_tok[:, :, :, :].rearrange("p a b m -> p (a b m)"), A[2][:, :], ACT.Copy).then_inc(kt_ok, 1)
                act.wait_ge(ls_ok, s + 1)
                a.activation(ex[:, :, :], ls[:, :, :], ACT.Exp).then_inc(ex_ok, 1)
                if not last:
                    token_rstd(s + 1)
                act.wait_ge(pv_ps, NGROUP * s + NGROUP // 2)
                a.activation(sq[:, 0, :], O[0][:, :], ACT.Square).then_inc(sq_ok, 1)
                head_rstd(s, 0)
                heads_hi(s, 0)
                if not last:
                    front(s + 1)
                act.wait_ge(pv_ps, NGROUP * s + NGROUP)
                a.activation(sq[:, 1, :], O[1][:, :], ACT.Square).then_inc(sq_ok, 1)
                head_rstd(s, 1)
                heads_hi(s, 1)
                if not last:
                    second_maps(s + 1)

            token_rstd(0)
            front(0)
            second_maps(0)
            with act.Fori(0, NBLK - 1) as s:
                block_step(s, False)
            block_step(NBLK - 1, True)

            done = act.alloc_register("act_tiles")
            act.reg_mov(done, 0)

            def tokens_hi(n):
                act.wait_ge(xg_free, n + 2)
                a.activation(gT_hi[:, :, :].rearrange("p c t -> p (c t)"), A[0][:, :], ACT.Copy).then_inc(ghi_ok, 1)

            tokens_hi(0)
            with act.Fori(0, NE // 2) as ep:
                for par in range(2):
                    n = act.value_load(n_tiles[0:1, bass.ds(ep * 2 + par, 1)], min_val=1, max_val=MAX_TILES)
                    with act.Fori(0, n):
                        t = act.snap(done, min_val=0, max_val=NE * MAX_TILES - 1)
                        for ic in range(IC):
                            act.wait_ge(gu_ps, t * IC + (ic + 1))
                            a.activation(sg[:, ic, :], bank_gu(ic)[:, 0:FT], ACT.Silu).then_inc(silu_ok, 1)
                            act.wait_ge(h_free, t * IC + (ic + 1 + IC))
                            a.activation(h_hi[:, ic, :], h[:, ic, :], ACT.Copy).then_inc(hhi_ok, 1)
                        tokens_hi(t + 1)
                        act.wait_ge(y_ps, t * SUB + 1)
                        act.wait_ge(scattered, (t + 3) * (SUB * DMA))
                        a.activation(ybuf[:, 0, :], O[0][:, 0:D], ACT.Copy,
                                     scale=w_tok[:, bass.ds(t * (SUB * NE) + (ep * 2 + par), 1)]).then_inc(ya_ok, 1)
                        act.reg_add(done, done, 1)

        @block.vector
        def _(dve):
            v = nc.vector
            c0 = Chain(dve, setup_dve)
            dve.wait_ge(loads, 3 * DMA)
            dve.wait_ge(masks, 1)
            for f in range(4):
                v.tensor_tensor(feat[:, f, :].rearrange("p (h d) -> p h d", h=HH), head_mask[:, :, :],
                                smalls[:, f * DK:(f + 1) * DK].unsqueeze(1).to_broadcast([P, HH, DK]),
                                ALU.mult).then_inc(feat_ok, 1)
            for par in range(2):
                last = v.tensor_reduce(parity[:, par:par + 1], head_mask[:, par:HH:2, 0:1].rearrange("p h d -> p d h"),
                                       axis=X_AXIS, op=ALU.add)
            c0.link(last)
            v.tensor_scalar(parity_b[:, :], parity[:, :], smalls[:, 4 * DK + 3:4 * DK + 4], None, ALU.mult)
            v.tensor_scalar(bq2[:, :], smalls[:, 4 * DK + 1:4 * DK + 2], DK ** -0.5, None, ALU.mult)
            for c in range(KC):
                last = v.tensor_scalar(wo_raw[:, c, :], wo_raw[:, c, :], smalls[:, 4 * DK + 4:4 * DK + 5], None,
                                       ALU.mult)
            c0.link(last)
            v.tensor_copy(wvr_hi[:, :, :], wvr_raw)
            c0.link(v.tensor_copy(wo_hi[:, :, :], wo_raw))
            v.tensor_tensor(wvr_lo[:, :, :], wvr_raw, wvr_hi[:, :, :].bitcast(F32), ALU.subtract)
            v.tensor_tensor(wo_lo[:, :, :], wo_raw, wo_hi[:, :, :].bitcast(F32), ALU.subtract).then_inc(split_ok, 1)
            for f in range(4):
                dve.wait_ge(setup_act, f + 1)
                last = v.tensor_tensor(wqk_lo[:, f, :, :].rearrange("p c n -> p (c n)"), A[f][:, :],
                                       wqk_hi[:, f, :, :].rearrange("p c n -> p (c n)").bitcast(F32), ALU.subtract)
                last.then_inc(fused_ok, 1)
            v.memset(mx[:, :], 0.0).then_inc(o_free, 2)
            chain_reg = dve.alloc_register("dve_base")
            dve.reg_mov(chain_reg, 0)

            def norm_stats(s, chain):
                dve.wait_ge(x_in, DMA * s + DMA)
                for t in range(TT):
                    last = v.bn_stats(stats[:, t, :], xa[:, t, :])
                chain.link(last)
                dve.sem_inc(dve_gate, 1)
                for t in range(TT):
                    last = v.bn_aggr(mv[:, t, :], stats[:, t, :])
                chain.link(last)
                v.tensor_scalar(var_eps[:, :], mv[:, :, 1], LN_EPS, None, ALU.add).then_inc(var_ok, 1)

            def norm_refine(s, chain):
                dve.wait_ge(rs0_ok, s + 1)
                chain.link(v.tensor_tensor(newton[:, :], rstd_x[:, :], rstd_x[:, :], ALU.mult))
                chain.link(v.tensor_tensor(newton[:, :], newton[:, :], var_eps[:, :], ALU.mult))
                chain.link(v.tensor_scalar(newton[:, :], newton[:, :], -0.5, 1.5, ALU.mult, ALU.add))
                chain.link(v.tensor_tensor(rstd_x[:, :], rstd_x[:, :], newton[:, :], ALU.mult))

            def norm_apply(s, first=False):
                if not first:
                    dve.wait_ge(table_in, DMA * s)
                    dve.wait_ge(xt_ps, KC * s)
                for t in range(TT):
                    last = v.tensor_scalar(xna[:, t, 0:D], xa[:, t, :], mv[:, t, 0:1], rstd_x[:, t:t + 1],
                                           ALU.subtract, ALU.mult)
                last.then_inc(xn_ok, 1)

            def front_tail(s):
                for c in range(KC):
                    dve.wait_ge(xhi_ok, KC * s + c + 1)
                    v.tensor_tensor(xT_lo[:, c, :], S[c][:, :], xT_hi[:, c, :].bitcast(F32), ALU.subtract).then_inc(xlo_ok, 1)

            def logits_out(s):
                dve.wait_ge(v_ok, TT * s + 2)
                v.tensor_copy(lg[:, 0:2, :], A_all[:, 2:4, D:AUG])
                dve.wait_ge(v_ok, TT * s + 4)
                v.tensor_copy(lg[:, 2:4, :], A_all[:, 0:2, D:AUG]).then_inc(lg_ok, 1)

            def queries_keys(s):
                for half in range(2):
                    dve.wait_ge(t2_ok, 6 * s + 3 * half + 1)
                    v.scalar_tensor_tensor(q[:, half, :], A[0][:, :], smalls[:, 4 * DK:4 * DK + 1], t2q[:, half, :],
                                           ALU.add, ALU.mult).then_inc(qk_ok, 1)
                    for par in range(2):
                        dve.wait_ge(t2_ok, 6 * s + 3 * half + 2 + par)
                        v.scalar_tensor_tensor(kz[:, half, par, :], A[2][:, :], smalls[:, 4 * DK + 2:4 * DK + 3],
                                               t2k[:, half, par, :], ALU.add, ALU.mult).then_inc(qk_ok, 1)

            def masked_scores(s, i):
                dve.wait_ge(s_ps, NGROUP * s + i + 1)
                v.tensor_tensor(s_sb[:, i % NS, :, :], scores_banks[i % NS][:, :].rearrange("p (n c) -> p n c", n=4),
                                causal[:, :].unsqueeze(1).to_broadcast([P, 4, P]), ALU.mult).then_inc(s_ok, 1)

            def softmax_head(s, chain):
                dve.wait_ge(lg_ok, s + 1)
                chain.link(v.tensor_reduce(mx[:, :], lg[:, :, :], axis=X_AXIS, op=ALU.max))
                v.tensor_tensor(ls[:, :, :], lg[:, :, :], mx[:, :].unsqueeze(2).to_broadcast([P, TT, NE]),
                                ALU.subtract).then_inc(ls_ok, 1)

            def softmax_tail(s, chain):
                dve.wait_ge(ex_ok, s + 1)
                chain.link(v.tensor_reduce(sm[:, :], ex[:, :, :], axis=X_AXIS, op=ALU.add))
                chain.link(v.reciprocal(sm[:, :], sm[:, :]))
                chain.link(v.tensor_tensor(pr[:, :, :], ex[:, :, :], sm[:, :].unsqueeze(2).to_broadcast([P, TT, NE]),
                                           ALU.mult))

            def ranked_before(chain):
                pf = pr[:, :, :].unsqueeze(2).to_broadcast([P, TT, NE, NE])
                pe = pr[:, :, :].unsqueeze(3).to_broadcast([P, TT, NE, NE])
                v.tensor_tensor(c_gt[:, :, :, :], pf, pe, ALU.is_gt)
                chain.link(v.tensor_tensor(c_eq[:, :, :, :], pf, pe, ALU.is_equal))
                chain.link(v.tensor_tensor(c_eq[:, :, :, :], c_eq[:, :, :, :],
                                           lower_e[:, :, :].unsqueeze(1).to_broadcast([P, TT, NE, NE]), ALU.mult))
                chain.link(v.tensor_tensor(c_gt[:, :, :, :], c_gt[:, :, :, :], c_eq[:, :, :, :], ALU.add))
                chain.link(v.tensor_tensor(c_gt[:, :, :, :], c_gt[:, :, :, :], pf, ALU.mult))

            def choose(s, chain):
                chain.link(v.tensor_reduce(cum[:, :, :], c_gt[:, :, :, :], axis=X_AXIS, op=ALU.add))
                chain.link(v.tensor_scalar(keep[:, :, :], cum[:, :, :], TOP_P, None, ALU.is_le))
                v.tensor_copy(sel[:, :, :], keep[:, :, :]).then_inc(sel_ok, 1)
                v.tensor_tensor(xna[:, :, D:AUG], pr[:, :, :], keep[:, :, :], ALU.mult).then_inc(w_ok, 1)

            def slots(s, chain):
                dve.wait_ge(rank_ps, s + 1)
                for t in range(TT):
                    chain.link(v.tensor_tensor(base[:, t + 1, :], base[:, t, :],
                                               A[2][:, TT * NE + t * NE:TT * NE + (t + 1) * NE], ALU.add))
                v.tensor_tensor(slot[:, :, :], A[2][:, 0:TT * NE].rearrange("p (t e) -> p t e", t=TT),
                                base[:, 0:TT, :], ALU.add).then_inc(rank_ok, 1)
                chain.link(v.tensor_scalar(keep[:, :, :], keep[:, :, :], -1.0, 1.0, ALU.mult, ALU.add))
                chain.link(v.tensor_tensor(keep[:, :, :], keep[:, :, :],
                                           from_end[:, :].unsqueeze(2).to_broadcast([P, TT, NE]), ALU.mult))
                dve.wait_ge(rank_ok, s + 1)
                chain.link(v.tensor_tensor(slot[:, :, :], slot[:, :, :], keep[:, :, :], ALU.add))
                chain.link(v.tensor_copy(slot_i[:, :, :], slot[:, :, :]))
                chain.link(v.tensor_scalar(lo_i[:, :, :], slot_i[:, :, :], P - 1, None, ALU.bitwise_and))
                chain.link(v.tensor_copy(slot_lo[:, :, :], lo_i[:, :, :]))
                chain.link(v.tensor_tensor(slot_hi[:, :, :], slot[:, :, :], slot_lo[:, :, :], ALU.subtract))
                n = TT * NE
                hi = slot_hi[:, :, :].rearrange("p t e -> p (t e)")
                v.tensor_tensor(oh_hi[:, :, :], hi_iota[:, :].unsqueeze(1).to_broadcast([P, n, NT // P]),
                                hi.unsqueeze(2).to_broadcast([P, n, NT // P]), ALU.is_equal).then_inc(slot_ok, 1)
                v.tensor_scalar(from_end[:, :], from_end[:, :], float(-BLK), None, ALU.add)
                chain.link(v.tensor_copy(base[:, 0, :], base[:, TT, :]))

            def one_hot(s, t):
                ins = v.tensor_tensor(oh_lo[:, t * NE:(t + 1) * NE, :], lo_iota[:, :].unsqueeze(1).to_broadcast([P, NE, P]),
                                      slot_lo[:, t, :].unsqueeze(2).to_broadcast([P, NE, P]), ALU.is_equal)
                if t == TT - 1:
                    ins.then_inc(lo_ok, 1)

            def head_norm(s, half, chain):
                dve.wait_ge(ro_ok, 2 * s + half + 1)
                v.tensor_tensor(on[:, half, :], O[half][:, :], rstd_o[:, half, :], ALU.mult).then_inc(on_ok, 1)

            def block_step(s, last):
                chain = Chain(dve, dve_step, dve.snap(chain_reg))
                logits_out(s)
                for i in range(NGROUP):
                    masked_scores(s, i)
                    if i == 1:
                        dve.wait_ge(kv_ps, s + 1)
                        v.tensor_tensor(kv[:, :, :, :].rearrange("p a b m -> p (a b) m"),
                                        A[3][:, :].rearrange("p (n m) -> p n m", n=4),
                                        head_mask[:, :, :].rearrange("p h d -> p (h d)").unsqueeze(1).to_broadcast([P, 4, P]),
                                        ALU.mult).then_inc(kv_ok, 1)
                    if i == 2:
                        softmax_head(s, chain)
                    if i == 3:
                        softmax_tail(s, chain)
                    if i == 4:
                        ranked_before(chain)
                    if i == 5:
                        choose(s, chain)
                    if i == 6 and not last:
                        norm_stats(s + 1, chain)
                    if i == 7:
                        slots(s, chain)
                    if i == 8 and not last:
                        norm_refine(s + 1, chain)
                    if 9 <= i < 9 + TT:
                        one_hot(s, i - 9)
                    if i == 13 and not last:
                        norm_apply(s + 1)
                    if i == 14:
                        head_norm(s, 0, chain)
                if not last:
                    front_tail(s + 1)
                dve.wait_ge(idx_ps, s + 1)
                v.tensor_tensor(idx_acc[:, :, :, :].rearrange("p e a n -> p (e a n)"),
                                A[3][:, :], idx_acc[:, :, :, :].rearrange("p e a n -> p (e a n)"),
                                ALU.add).then_inc(idx_ok, 1)
                head_norm(s, 1, chain)
                if not last:
                    queries_keys(s + 1)
                dve.wait_ge(xr_in, DMA * s + DMA)
                dve.wait_ge(yout_free, DMA * s + DMA)
                for i in range(2):
                    dve.wait_ge(wo_ps, 2 * s + i + 1)
                    v.tensor_tensor(yout[:, 2 * i:2 * i + 2, :], O[i][:, :].rearrange("p (t d) -> p t d", t=2),
                                    xr[:, 2 * i:2 * i + 2, :], ALU.add).then_inc(y_ok, 1)
                chain.link(v.memset(stats[:, 0, 0:1], 0.0))
                v.memset(stats[:, 0, 1:2], 0.0).then_inc(o_free, 2)
                dve.reg_add(chain_reg, chain_reg, chain.n)

            chain = Chain(dve, dve_step, None)
            norm_stats(0, chain)
            norm_refine(0, chain)
            norm_apply(0, True)
            front_tail(0)
            queries_keys(0)
            dve.reg_mov(chain_reg, chain.n)
            with dve.Fori(0, NBLK - 1) as s:
                block_step(s, False)
            block_step(NBLK - 1, True)

            chain = Chain(dve, dve_step, dve.snap(chain_reg))
            dve.wait_ge(idx_ok, NBLK)
            dve.wait_ge(table_in, DMA * NBLK)
            dve.wait_ge(yout_free, DMA * (NBLK + 1))
            chain.link(v.scalar_tensor_tensor(idx_f[:, :, :], idx_acc[:, :, 1, :], float(P), idx_acc[:, :, 0, :],
                                              ALU.mult, ALU.add))
            v.tensor_copy(idx_all[:, :], idx_f[:, :, :].rearrange("p e n -> p (e n)"))
            chain.link(v.tensor_scalar(cum[0:1, 0, :], base[0:1, 0, :], float(FT - 1), None, ALU.add))
            chain.link(v.tensor_copy(cnt_i[:, :], cum[0:1, 0, :]))
            chain.link(v.tensor_scalar(cnt_i[:, :], cnt_i[:, :], FT.bit_length() - 1, None, ALU.arith_shift_right))
            chain.link(v.tensor_scalar(n_tiles[:, :], cnt_i[:, :], 1, None, ALU.max))
            v.memset(ybuf[:, :, :], 0.0).then_inc(ya_ok, 2)
            v.memset(h[:, :, 0:1], 0.0).then_inc(h_free, IC)
            v.memset(h[:, :, 1:2], 0.0).then_inc(yd_ok, 2)
            v.memset(h[:, :, 3:4], 0.0).then_inc(wt_ok, 1)
            v.memset(h[:, :, 4:5], 0.0).then_inc(tab_ok, 1)

            done = dve.alloc_register("dve_tiles")
            dve.reg_mov(done, 0)

            def tokens_lo(n):
                dve.wait_ge(ghi_ok, n + 1)
                v.tensor_tensor(gT_lo[:, :, :].rearrange("p c t -> p (c t)"), A[0][:, :],
                                gT_hi[:, :, :].rearrange("p c t -> p (c t)").bitcast(F32), ALU.subtract).then_inc(glo_ok, 1)
                v.tensor_copy(w_tok[:, bass.ds(n * (SUB * NE), SUB * NE)].rearrange("p (a e) -> p a e", a=SUB),
                              xg[:, :, D:AUG]).then_inc(wt_ok, 1)

            tokens_lo(0)
            with dve.Fori(0, NE // 2) as ep:
                for par in range(2):
                    n = dve.value_load(n_tiles[0:1, bass.ds(ep * 2 + par, 1)], min_val=1, max_val=MAX_TILES)
                    with dve.Fori(0, n):
                        t = dve.snap(done, min_val=0, max_val=NE * MAX_TILES - 1)
                        for ic in range(IC):
                            dve.wait_ge(silu_ok, t * IC + (ic + 1))
                            v.tensor_tensor(h[:, ic, :], sg[:, ic, :], bank_gu(ic)[:, FT:2 * FT], ALU.mult).then_inc(h_free, 1)
                            dve.wait_ge(hhi_ok, t * IC + (ic + 1))
                            v.tensor_tensor(h_lo[:, ic, :], h[:, ic, :], h_hi[:, ic, :].bitcast(F32),
                                            ALU.subtract).then_inc(hlo_ok, 1)
                        tokens_lo(t + 1)
                        dve.wait_ge(y_ps, t * SUB + 2)
                        dve.wait_ge(scattered, (t + 3) * (SUB * DMA))
                        v.tensor_scalar(ybuf[:, 1, :], O[1][:, 0:D],
                                        w_tok[:, bass.ds(t * (SUB * NE) + (NE + par) + ep * 2, 1)], None,
                                        ALU.mult).then_inc(yd_ok, 1)
                        dve.reg_add(done, done, 1)

        @block.tensor
        def _(pe):
            mm = nc.tensor.matmul

            def product(out_ap, l_hi, l_lo, r_hi, r_lo, n, k):
                mm(out_ap, l_hi, r_hi, start=(k == 0), stop=False)
                mm(out_ap, l_hi, r_lo, start=False, stop=False)
                return mm(out_ap, l_lo, r_hi, start=False, stop=(k == n - 1))

            pe.wait_ge(natural, DMA)
            for f in range(4):
                pe.wait_ge(feat_ok, f + 1)
                for kc in range(KC):
                    for hc in range(2):
                        last = mm(A[f][:, kc * D + hc * P:kc * D + hc * P + P], nat[:, f // 2, hc, kc * P:(kc + 1) * P],
                                  feat[:, f, :], start=True, stop=True)
                last.then_inc(fused_ps, 1)
            pe.wait_ge(fused_ps, 4)
            pe.nop().then_inc(split_ok, 1)
            pe.wait_ge(fused_ok, 4)

            def transposes(s, c):
                pe.wait_ge(xn_ok, s + 1)
                for t in range(TT):
                    last = nc.tensor.transpose(S[c][:, t * P:(t + 1) * P], xna[:, t, c * P:(c + 1) * P], ident[:, :])
                last.then_inc(xt_ps, 1)

            def project(bank, f, half):
                w = slice(half * P, (half + 1) * P)
                for c in range(KC):
                    last = product(bank[:, :], wqk_hi[:, f, c, w], wqk_lo[:, f, c, w], xT_hi[:, c, :], xT_lo[:, c, :], KC, c)
                return last

            def projections(s, first=False):
                pe.wait_ge(xlo_ok, KC * s + KC)
                for half in range(2):
                    if half == 1:
                        pe.wait_ge(qk_ok, 6 * s + 1)
                    project(A[0], 0, half)
                    project(A[1], 1, half).then_inc(proj_ps, 1)
                    if half == 1:
                        pe.wait_ge(qk_ok, 6 * s + 3)
                    elif not first:
                        pe.wait_ge(ln_o_ok, 2 * s)
                        pe.wait_ge(idx_ok, s)
                    project(A[2], 2, half)
                    project(A[3], 3, half).then_inc(proj_ps, 1)

            def scores(s, i):
                half, b, g = i // 8, i // 4 % 2, i % 4
                if i % 8 == 0:
                    pe.wait_ge(qk_ok, 6 * s + 3 * half + 3)
                rows = slice(32 * g, 32 * g + 32)
                for t in range(2):
                    tok = slice((2 * b + t) * P, (2 * b + t + 1) * P)
                    for par in range(2):
                        n = 2 * t + par
                        last = mm(scores_banks[i % NS][:, n * P:(n + 1) * P], kz[rows, half, par, tok], q[rows, half, tok],
                                  start=True, stop=True, tile_position=(32 * g, 0))
                last.then_inc(s_ps, 1)

            def values(s, i):
                half, b, g = i // 8, i // 4 % 2, i % 4
                if i == 0:
                    pe.wait_ge(kv_ok, s + 1)
                    pe.wait_ge(o_free, 2 * s + 2)
                if i % 4 == 0:
                    tok = slice((2 * b + 1) * P, (2 * b + 2) * P)
                    mm(O[half][:, tok], kv[:, half, b, :], q[:, half, tok], start=True, stop=True, skip_group_check=True)
                pe.wait_ge(s_ok, NGROUP * s + i + 1)
                for t in range(2):
                    tok = slice((2 * b + t) * P, (2 * b + t + 1) * P)
                    for par in range(2):
                        w = vz[:, 2 * b + t, half * PAIRS + g, 2 * par:2 * par + 2, :].rearrange("p a d -> p (a d)")
                        last = mm(O[half][32 * g:32 * g + 32, tok], w, s_sb[:, i % NS, 2 * t + par, :],
                                  start=False, stop=True, skip_group_check=True, tile_position=(0, 32 * g))
                last.then_inc(pv_ps, 1)

            def mean_squares(s, half):
                pe.wait_ge(sq_ok, 2 * s + half + 1)
                if half == 1:
                    pe.wait_ge(rank_ok, s + 1)
                mm(A[3 - half][:, :], head_mean[:, :], sq[:, half, :], start=True, stop=True).then_inc(ms_ps, 1)

            def slot_tokens(s):
                pe.wait_ge(ln_o_ok, 2 * s + 1)
                pe.wait_ge(oh_ok, s + 1)
                pe.wait_ge(lo_ok, s + 1)
                for e in range(NE):
                    for t in range(TT):
                        n = t * NE + e
                        o = mm(A[3][:, e * 64:(e + 1) * 64], oh_lo[:, n, :],
                               oh_rhs[:, n, :, :].rearrange("p a n -> p (a n)"), start=(t == 0), stop=(t == TT - 1))
                o.then_inc(idx_ps, 1)

            def output_projection(s):
                pe.wait_ge(onlo_ok, 2 * s + 2)
                for t in range(TT):
                    tok = slice(t * P, (t + 1) * P)
                    for half in range(2):
                        o = product(O[t // 2][:, t % 2 * D:(t % 2 + 1) * D], on_hi[:, half, tok], on_lo[:, half, tok],
                                    wo_hi[:, half, :], wo_lo[:, half, :], 2, half)
                    if t % 2:
                        o.then_inc(wo_ps, 1)

            def block_step(s, last):
                for t in range(TT):
                    tok = slice(t * P, (t + 1) * P)
                    if t == 0:
                        pe.wait_ge(qk_ok, 6 * s + 6)
                    for c in range(KC):
                        o = product(values_banks[t][:, 0:AUG], xT_hi[:, c, tok], xT_lo[:, c, tok],
                                    wvr_hi[:, c, :], wvr_lo[:, c, :], KC, c)
                    o.then_inc(v_ps, 1)
                scores(s, 0)
                pe.wait_ge(kf_ok, 2 * s + 2)
                pe.wait_ge(v_ok, TT * s + TT)
                pe.wait_ge(lg_ok, s + 1)
                for half in range(2):
                    for b in range(2):
                        o = nc.tensor.transpose(A[2][:, (2 * half + b) * P:(2 * half + b + 1) * P], kf[:, half, b, :],
                                                ident[:, :])
                o.then_inc(kt_ps, 1)
                scores(s, 1)
                scores(s, 2)
                pe.wait_ge(kt_ok, s + 1)
                for half in range(2):
                    for b in range(2):
                        rhs = vz[:, 2 * b, half * PAIRS:(half + 1) * PAIRS, 0:4:3, :]
                        o = mm(A[3][:, (2 * half + b) * P:(2 * half + b + 1) * P], k_tok[:, half, b, :], rhs,
                               start=True, stop=True)
                o.then_inc(kv_ps, 1)
                scores(s, 3)
                for i in range(NGROUP):
                    values(s, i)
                    if i + NS < NGROUP:
                        scores(s, i + NS)
                    if i == 3:
                        pe.wait_ge(sel_ok, s + 1)
                        chosen = sel[:, :, :].rearrange("p t e -> p (t e)")
                        mm(A[2][:, 0:TT * NE], before[:, :], chosen, start=True, stop=True)
                        mm(A[2][:, TT * NE:2 * TT * NE], ones_bf[:, :], chosen, start=True, stop=True).then_inc(rank_ps, 1)
                    if i == 9:
                        mean_squares(s, 0)
                    if 12 <= i < 12 + KC and not last:
                        transposes(s + 1, i - 12)
                slot_tokens(s)
                mean_squares(s, 1)
                if not last:
                    projections(s + 1)
                output_projection(s)

            for c in range(KC):
                transposes(0, c)
            projections(0, True)
            with pe.Fori(0, NBLK - 1) as s:
                block_step(s, False)
            block_step(NBLK - 1, True)

            pe.nop().then_inc(xg_free, 1)
            pe.nop().then_inc(w_free, 1)
            pe.wait_ge(tab_ok, 1)
            pe.wait_ge(o_free, 2 * NBLK + 2)
            done = pe.alloc_register("pe_tiles")
            pe.reg_mov(done, 0)

            def tokens(n):
                pe.wait_ge(gathered, n * (SUB * DMA) + SUB * DMA)
                for c in range(KC):
                    for sub in range(SUB):
                        last = nc.tensor.transpose(A[0][:, c * FT + sub * P:c * FT + (sub + 1) * P],
                                                   xg[:, sub, c * P:(c + 1) * P], ident[:, :])
                last.then_inc(xg_free, 1)

            tokens(0)
            pe.nop()
            with pe.Fori(0, NE // 2) as ep:
                for par in range(2):
                    n = pe.value_load(n_tiles[0:1, bass.ds(ep * 2 + par, 1)], min_val=1, max_val=MAX_TILES)
                    pe.wait_ge(wsplit, ep * (2 * PIECES) + PIECES * (par + 1))
                    pe.sem_inc(pe_gate, 1)
                    with pe.Fori(0, n):
                        t = pe.snap(done)
                        pe.wait_ge(glo_ok, t + 1)
                        for ic in range(IC):
                            pe.wait_ge(h_free, t * IC + (ic + 1))
                            for m in range(2):
                                for c in range(KC):
                                    w = slice(m * KC * NI + c * NI + ic * P, m * KC * NI + c * NI + (ic + 1) * P)
                                    last = product(bank_gu(ic)[:, m * FT:(m + 1) * FT], w_hi[par][:, w], w_lo[par][:, w],
                                                   gT_hi[:, c, :], gT_lo[:, c, :], KC, c)
                            last.then_inc(gu_ps, 1)
                        tokens(t + 1)
                        pe.wait_ge(ya_ok, t + 2)
                        pe.wait_ge(yd_ok, t + 2)
                        for ic in range(IC):
                            pe.wait_ge(hlo_ok, t * IC + (ic + 1))
                            w = slice(down0 + ic * D, down0 + (ic + 1) * D)
                            for sub in range(SUB):
                                tok = slice(sub * P, (sub + 1) * P)
                                last = product(O[sub][:, 0:D], h_hi[:, ic, tok], h_lo[:, ic, tok],
                                               w_hi[par][:, w], w_lo[par][:, w], IC, ic)
                                if ic == IC - 1:
                                    last.then_inc(y_ps, 1)
                        pe.reg_add(done, done, 1)
                    pe.wait_ge(y_ps, pe.snap(done) * SUB)
                    pe.nop().then_inc(w_free, 1)


def kernel(**inputs):
    import numpy as np
    import concourse.bacc as bacc
    from concourse.bass_utils import run_bass_kernel_spmd

    a = {n.replace("L0_attn_", "").replace("L0_ffn_", ""): np.asarray(v) for n, v in inputs.items()}
    by_row = lambda w: w.reshape(KC, P, -1).transpose(1, 0, 2)
    heads = lambda v: np.tile(v, (HH, 1))
    arrays = {
        "x": a["x"].reshape(NT, D),
        "wqk_nat": np.stack([by_row(a["wq"]), by_row(a["wk"])], 1),
        "small": np.concatenate([heads(a[n].T) for n in ("fq1_w", "fq2_w", "fk1_w", "fk2_w")]
                                + [heads(a[n][:, None]) for n in ("fq1_b", "fq2_b", "fk1_b", "fk2_b", "norm_w")], 1),
        "wvr": by_row(np.concatenate([a["wv"].T, a["router_w"].T], 1)),
        "wo": by_row(a["wo"].T),
        "wffn": np.concatenate([
            w.transpose(0, 2, 1).reshape(NE, -1, P, w.shape[1]).transpose(0, 2, 1, 3).reshape(NE, P, -1)
            for w in (a["gate_w"], a["up_w"], a["down_w"])], 2),
    }
    arrays = {n: np.ascontiguousarray(v) for n, v in arrays.items()}
    nc = bacc.Bacc("TRN2", target_bir_lowering=False, num_devices=1)
    args = {n: nc.dram_tensor(n, v.shape, mybir.dt.from_np(v.dtype), kind="ExternalInput").ap()
            for n, v in arrays.items()}
    out = nc.dram_tensor("out", [NT, D], F32, kind="ExternalOutput").ap()
    build(nc, out=out, **args)
    r = run_bass_kernel_spmd(nc, [arrays], core_ids=[0])
    return r.results[0]["out"].reshape(inputs["L0_attn_x"].shape)
```

```python
from contextlib import ExitStack

import concourse.bass as bass
from concourse import mybir
from concourse.alu_op_type import AluOpType as ALU

F32 = mybir.dt.float32
F32R = mybir.dt.float32r
BF16 = mybir.dt.bfloat16
I32 = mybir.dt.int32
U32 = mybir.dt.uint32
ACT = mybir.ActivationFunctionType
X_AXIS = mybir.AxisListType.X

P = 128
NT = 4096
D = 256
KC = D // P
BLK = 512
NBLK = NT // BLK
TT = BLK // P
DK = 16
HH = P // DK
PAIRS = HH // 2
NE = 8
NI = 512
IC = NI // P
TOP_P = 0.9
LN_EPS = 1e-5
RMS_EPS = 1e-5
AUG = D + NE
FT = 256
SUB = FT // P
MAX_TILES = NT // FT
WE = KC * NI * 2 + IC * D
PIECES = 4
PW = WE // PIECES
NGROUP = 2 * 2 * PAIRS
NS = 2
LAG = 2
DMA = 16


def group(i):
    return i // (2 * PAIRS), i // PAIRS % 2, i % PAIRS


class Chain:

    def __init__(self, eng, sem, base=None):
        self.eng, self.sem, self.base, self.n = eng, sem, base, 0

    def link(self, ins):
        ins.then_inc(self.sem, 1)
        self.n += 1
        self.eng.wait_ge(self.sem, self.n if self.base is None else self.base + self.n)


class TileCounts:

    def __init__(self, eng, n_tiles):
        self.eng, self.n_tiles = eng, n_tiles
        self.present = eng.alloc_register("tiles_of_expert")
        self.following = eng.alloc_register("tiles_of_next")
        self.load_next(0)
        self.step()

    def load_next(self, e):
        n = self.eng.value_load(self.n_tiles[0:1, bass.ds(e, 1)], min_val=1, max_val=MAX_TILES)
        self.eng.reg_mov(self.following, n)

    def now(self):
        return self.eng.snap(self.present, min_val=1, max_val=MAX_TILES)

    def step(self):
        self.eng.reg_mov(self.present, self.following)


def build(nc, x, wqk_nat, small, wvr, wo, wffn, out):
    ctx = ExitStack()
    with ctx:
        def sb(name, shape, dt=F32):
            return ctx.enter_context(nc.sbuf_tensor(name, shape, dt))

        def ps(name, shape, dt=F32):
            return ctx.enter_context(nc.psum_tensor(name, shape, dt))

        def sem(name):
            return ctx.enter_context(nc.semaphore(name))

        x_blk = x.rearrange("(s t p) d -> s p t d", t=TT, p=P)
        out_blk = out.rearrange("(s t p) d -> s p t d", t=TT, p=P)
        table = nc.dram_tensor("gather_table", [NT, AUG], F32, kind="Internal").ap()
        table_blk = table.rearrange("(s t p) d -> s p t d", t=TT, p=P)

        ident = sb("ident", [P, P])
        head_mask = sb("head_mask", [P, HH, DK])
        head_mean = sb("head_mean", [P, P])
        causal = sb("causal", [P, P])
        before = sb("before", [P, P], BF16)
        ones_bf = sb("ones_bf", [P, P], BF16)
        lo_iota = sb("lo_iota", [P, P])
        hi_iota = sb("hi_iota", [P, NT // P])
        part = sb("part", [P, 1])
        lower_e = sb("lower_e", [P, NE, NE])
        parity = sb("parity", [P, 2])
        parity_b = sb("parity_b", [P, 2])
        eps = sb("eps", [P, 1])
        bq2 = sb("bq2", [P, 1])
        smalls = sb("smalls", [P, 4 * DK + 5])
        wqk_hi = sb("wqk_hi", [P, 4, KC, D], F32R)
        wqk_lo = sb("wqk_lo", [P, 4, KC, D], F32R)
        wvr_hi = sb("wvr_hi", [P, KC, AUG], F32R)
        wvr_lo = sb("wvr_lo", [P, KC, AUG], F32R)
        wo_hi = sb("wo_hi", [P, KC, D], F32R)
        wo_lo = sb("wo_lo", [P, KC, D], F32R)
        feat = sb("feat", [P, 4, P])
        w_raw = sb("w_raw", [P, WE])
        w_hi = [sb(f"w_hi{i}", [P, WE], F32R) for i in range(2)]
        w_lo = [sb(f"w_lo{i}", [P, WE], F32R) for i in range(2)]
        base = sb("base", [P, TT + 1, NE])
        from_end = sb("from_end", [P, TT])
        tile_no = sb("tile_no", [P, TT])
        idx_acc = sb("idx_acc", [P, NE, 2, NT // P])
        idx_all = sb("idx_all", [P, NE * (NT // P)], U32)
        n_tiles = sb("n_tiles", [1, NE + 1], I32)

        ph1 = ExitStack()

        def sb1(name, shape, dt=F32):
            return ph1.enter_context(nc.sbuf_tensor(name, shape, dt))

        xa = sb1("xa", [P, TT, D])
        stats = sb1("stats", [P, TT, 6])
        mv = sb1("mv", [P, TT, 2])
        rstd_x = sb1("rstd_x", [P, TT])
        var_eps = sb1("var_eps", [P, TT])
        newton = sb1("newton", [P, TT])
        ln_x = sb1("ln_x", [P, TT])
        ln_o = sb1("ln_o", [P, 2, BLK])
        slot_i = sb1("slot_i", [P, TT, NE], I32)
        lo_i = sb1("lo_i", [P, TT, NE], I32)
        xna = sb1("xna", [P, TT, AUG])
        xT_hi = sb1("xT_hi", [P, KC, BLK], F32R)
        xT_lo = sb1("xT_lo", [P, KC, BLK], F32R)
        t2q = sb1("t2q", [P, 2, BLK])
        t2k = sb1("t2k", [P, 2, 2, BLK])
        q = sb1("q", [P, 2, BLK])
        kz = sb1("kz", [P, 2, 2, BLK])
        kf = sb1("kf", [P, 2, 2, P])
        k_tok = sb1("k_tok", [P, 2, 2, P])
        kv = sb1("kv", [P, 2, 2, P])
        vz = sb1("vz", [P, TT, 2 * PAIRS, 4, DK])
        s_sb = sb1("s_sb", [P, NS, 4, P])
        sq = sb1("sq", [P, 2, BLK])
        rstd_o = sb1("rstd_o", [P, 2, BLK])
        on = sb1("on", [P, 2, BLK])
        on_hi = sb1("on_hi", [P, 2, BLK], F32R)
        on_lo = sb1("on_lo", [P, 2, BLK], F32R)
        xr = sb1("xr", [P, TT, D])
        yout = sb1("yout", [P, TT, D])
        lg = sb1("lg", [P, TT, NE])
        mx = sb1("mx", [P, TT])
        ls = sb1("ls", [P, TT, NE])
        ex = sb1("ex", [P, TT, NE])
        sm = sb1("sm", [P, TT])
        pr = sb1("pr", [P, TT, NE])
        c_gt = sb1("c_gt", [P, TT, NE, NE])
        c_eq = sb1("c_eq", [P, TT, NE, NE])
        cum = sb1("cum", [P, TT, NE])
        keep = sb1("keep", [P, TT, NE])
        sel = sb1("sel", [P, TT, NE], BF16)
        slot = sb1("slot", [P, TT, NE])
        slot_lo = sb1("slot_lo", [P, TT, NE])
        slot_hi = sb1("slot_hi", [P, TT, NE])
        oh_lo = sb1("oh_lo", [P, TT * NE, P], BF16)
        oh_hi = sb1("oh_hi", [P, TT * NE, NT // P])
        oh_rhs = sb1("oh_rhs", [P, TT * NE, 2, NT // P], BF16)
        ph1.close()

        ph2 = ctx.enter_context(ExitStack())

        def sb2(name, shape, dt=F32):
            return ph2.enter_context(nc.sbuf_tensor(name, shape, dt))

        idx_f = sb2("idx_f", [P, NE, NT // P])
        cnt_i = sb2("cnt_i", [1, NE], I32)
        xg = sb2("xg", [P, SUB, AUG])
        g_idx = sb2("g_idx", [P, SUB], U32)
        s_idx = sb2("s_idx", [P, SUB], U32)
        gT_hi = sb2("gT_hi", [P, KC, FT], F32R)
        gT_lo = sb2("gT_lo", [P, KC, FT], F32R)
        sg = sb2("sg", [P, IC, FT])
        h = sb2("h", [P, IC, FT])
        h_hi = sb2("h_hi", [P, IC, FT], F32R)
        h_lo = sb2("h_lo", [P, IC, FT], F32R)
        ybuf = sb2("ybuf", [P, SUB, D])
        w_tok = sb2("w_tok", [P, (NE * MAX_TILES + 1) * SUB * NE])

        A = [ps(f"A{i}", [P, 512]) for i in range(4)]
        S = [ps(f"S{i}", [P, 512]) for i in range(2)]
        k_banks = [(A[0], A[2]), (A[3], A[0])]
        q_banks = [(A[1], A[3]), (A[2], A[1])]
        values_banks = [A[0], A[1], A[2], A[3]]
        kt_banks = [A[0], A[3]]
        wo_banks = [A[2], A[1]]
        rank_bank = idx_bank = A[0]
        ms_bank = A[1]
        xt_banks = [A[2], A[0]]
        scores_banks = S
        O = [ps(f"O{i}", [P, 512]) for i in range(2)]

        names = ("small_in vo_in natural masks counts feat_ok fused_ps fused_ok split_ok setup_dve setup_act "
                 "x_in xn_ok xt_ps xhi_ok xlo_ok lg_ok proj_ps t2_ok qk_ok v_ps v_ok kf_ok kt_ps kt_ok kv_ps kv_ok "
                 "s_ps s_ok pv_ps sq_ok ms_ps ro_ok var_ok rs0_ok ln_x_ok ln_o_ok on_ok onhi_ok onlo_ok wo_ps xr_in yout_free y_ok "
                 "ls_ok ex_ok sel_ok rank_ps rank_ok slot_ok lo_ok oh_ok idx_ps idx_ok w_ok table_in "
                 "dve_step pool_step tab_ok w_in wsplit "
                 "gathered xg_free ghi_ok glo_ok gu_ps silu_ok h_free hhi_ok hlo_ok y_ps ya_ok yd_ok "
                 "wt_ok scattered pool_gate dve_gate pe_gate act_gate whi_ok")
        sems = {n: sem(n) for n in names.split()}
        (small_in, vo_in, natural, masks, counts, feat_ok, fused_ps, fused_ok, split_ok, setup_dve, setup_act,
         x_in, xn_ok, xt_ps, xhi_ok, xlo_ok, lg_ok, proj_ps, t2_ok, qk_ok, v_ps, v_ok, kf_ok, kt_ps, kt_ok, kv_ps, kv_ok,
         s_ps, s_ok, pv_ps, sq_ok, ms_ps, ro_ok, var_ok, rs0_ok, ln_x_ok, ln_o_ok, on_ok, onhi_ok, onlo_ok, wo_ps, xr_in, yout_free, y_ok,
         ls_ok, ex_ok, sel_ok, rank_ps, rank_ok, slot_ok, lo_ok, oh_ok, idx_ps, idx_ok, w_ok, table_in,
         dve_step, pool_step, tab_ok, w_in, wsplit,
         gathered, xg_free, ghi_ok, glo_ok, gu_ps, silu_ok, h_free, hhi_ok, hlo_ok, y_ps, ya_ok, yd_ok,
         wt_ok, scattered, pool_gate, dve_gate, pe_gate, act_gate, whi_ok) = [sems[n] for n in names.split()]

        nat = w_raw[:, 0:2 * KC * D].rearrange("p (m c k) -> p m c k", m=2, c=KC)
        wvr_raw = w_raw[:, 2 * KC * D:2 * KC * D + KC * AUG].rearrange("p (c k) -> p c k", c=KC)
        wo_raw = w_raw[:, 2 * KC * D + KC * AUG:3 * KC * D + KC * AUG].rearrange("p (c k) -> p c k", c=KC)
        down0 = 2 * KC * NI

        def bank_gu(ic):
            return (A[1], A[2], A[3], S[0])[ic]

        block = ctx.enter_context(nc.Block())

        @block.sync
        def _(sp):
            sp.dma_start(xa[:, :, :], x_blk[0]).then_inc(x_in, DMA)
            sp.dma_start(smalls[:, :], small).then_inc(small_in, DMA)
            sp.dma_start(nat, wqk_nat).then_inc(natural, DMA)
            sp.dma_start(wvr_raw, wvr).then_inc(vo_in, DMA)
            sp.dma_start(wo_raw, wo).then_inc(vo_in, DMA)
            sp.wait_ge(split_ok, 2)
            sp.dma_start(w_raw[:, :], wffn[0]).then_inc(w_in, DMA)

            sp.wait_ge(xn_ok, 1)
            sp.dma_start(xa[:, :, :], x_blk[1]).then_inc(x_in, DMA)

            def first_half(s, first, more):
                if not first:
                    sp.wait_ge(y_ok, 2 * s)
                    sp.dma_start(xr[:, :, :], x_blk[s - 1]).then_inc(xr_in, DMA)
                sp.wait_ge(w_ok, s + 1)
                sp.dma_start(table_blk[s], xna[:, :, :]).then_inc(table_in, DMA)
                if not first:
                    sp.wait_ge(y_ok, 2 * s + 2)
                    sp.dma_start(out_blk[s - 1], yout[:, :, :]).then_inc(yout_free, DMA)
                if more:
                    sp.wait_ge(xn_ok, s + 2)
                    sp.dma_start(xa[:, :, :], x_blk[s + 2]).then_inc(x_in, DMA)

            def next_weights(e):
                sp.wait_ge(wsplit, PIECES * e)
                sp.dma_start(w_raw[:, :], wffn[e]).then_inc(w_in, DMA)

            first_half(0, True, True)
            with sp.Fori(0, NBLK - 3) as s:
                first_half(s + 1, False, True)
            first_half(NBLK - 2, False, False)
            first_half(NBLK - 1, False, False)
            sp.wait_ge(y_ok, 2 * NBLK)
            sp.dma_start(xr[:, :, :], x_blk[NBLK - 1]).then_inc(xr_in, DMA)
            next_weights(1)
            sp.wait_ge(y_ok, 2 * NBLK + 2)
            sp.dma_start(out_blk[NBLK - 1], yout[:, :, :]).then_inc(yout_free, DMA)
            for e in range(2, NE):
                next_weights(e)

        @block.gpsimd
        def _(pool):
            g = nc.gpsimd
            g.memset(ident[:, :], 0.0).then_inc(pool_step, 1)
            g.memset(head_mask[:, :, :], 1.0).then_inc(pool_step, 1)
            g.memset(causal[:, :], 1.0).then_inc(pool_step, 1)
            g.memset(before[:, :], 1.0).then_inc(pool_step, 1)
            g.memset(lower_e[:, :, :], 1.0).then_inc(pool_step, 1)
            pool.wait_ge(pool_step, 5)
            g.affine_select(out=ident[:, :], in_=ident[:, :], compare_op=ALU.not_equal, fill=1.0,
                            base=0, pattern=[[-1, P]], channel_multiplier=1).then_inc(pool_step, 1)
            g.affine_select(out=head_mask[:, :, :], in_=head_mask[:, :, :], compare_op=ALU.is_ge, fill=0.0,
                            base=0, pattern=[[-DK, HH], [0, DK]], channel_multiplier=1).then_inc(pool_step, 1)
            g.affine_select(out=causal[:, :], in_=causal[:, :], compare_op=ALU.is_ge, fill=0.0,
                            base=0, pattern=[[1, P]], channel_multiplier=-1).then_inc(pool_step, 1)
            g.affine_select(out=before[:, :], in_=before[:, :], compare_op=ALU.is_ge, fill=0.0,
                            base=-1, pattern=[[1, P]], channel_multiplier=-1).then_inc(pool_step, 1)
            g.affine_select(out=lower_e[:, :, :], in_=lower_e[:, :, :], compare_op=ALU.is_ge, fill=0.0,
                            base=-1, pattern=[[1, NE], [-1, NE]], channel_multiplier=0).then_inc(pool_step, 1)
            pool.wait_ge(pool_step, 10)
            g.affine_select(out=head_mask[:, :, :], in_=head_mask[:, :, :], compare_op=ALU.is_ge, fill=0.0,
                            base=DK - 1, pattern=[[DK, HH], [0, DK]], channel_multiplier=-1).then_inc(pool_step, 1)
            pool.wait_ge(pool_step, 11)
            g.tensor_scalar(head_mean[:, :], head_mask[:, :, :].rearrange("p h d -> p (h d)"), 1.0 / DK, None,
                            ALU.mult).then_inc(masks, 1)
            g.memset(ones_bf[:, :], 1.0)
            g.memset(eps[:, :], RMS_EPS)
            g.iota(lo_iota[:, :], pattern=[[1, P]], base=0, channel_multiplier=0, allow_small_or_imprecise_dtypes=True)
            g.iota(hi_iota[:, :], pattern=[[P, NT // P]], base=0, channel_multiplier=0,
                   allow_small_or_imprecise_dtypes=True)
            g.iota(part[:, :], pattern=[[0, 1]], base=0, channel_multiplier=1, allow_small_or_imprecise_dtypes=True)
            g.iota(from_end[:, :], pattern=[[-P, TT]], base=NT - 1, channel_multiplier=-1,
                   allow_small_or_imprecise_dtypes=True)
            g.iota(tile_no[:, :], pattern=[[1, TT]], base=0, channel_multiplier=0,
                   allow_small_or_imprecise_dtypes=True)
            g.memset(base[:, :, :], 0.0)
            g.memset(idx_acc[:, :, :, :], 0.0)
            g.memset(vz[:, :, :, :, :], 0.0).then_inc(counts, 1)
            g.memset(yout[:, 0, 0:1], 0.0).then_inc(yout_free, DMA)

            def first_keys(s, half):
                pool.wait_ge(qk_ok, 6 * s + (2, 6)[half])
                first = [kz[:, half, par, :].rearrange("p (b c m) -> p b c m", b=2, c=2)[:, :, 0, :]
                         for par in range(2)]
                g.tensor_tensor(kf[:, half, :, :], first[0], first[1], ALU.add).then_inc(kf_ok, 1)

            def outputs_low(s, half):
                pool.wait_ge(onhi_ok, 2 * s + half + 1)
                g.tensor_tensor(on_lo[:, half, :], on[:, half, :], on_hi[:, half, :].bitcast(F32),
                                ALU.subtract).then_inc(onlo_ok, 1)

            def low_piece(par, c0):
                whi = w_hi[par][:, bass.ds(c0, PW)]
                g.tensor_tensor(w_lo[par][:, bass.ds(c0, PW)], w_raw[:, bass.ds(c0, PW)], whi.bitcast(F32),
                                ALU.subtract).then_inc(wsplit, 1)

            def add_rows():
                for sub in range(SUB):
                    pool.indirect_dma_start(
                        out=out, out_offset=bass.IndirectOffsetOnAxis(ap=s_idx[:, sub:sub + 1], axis=0),
                        in_=ybuf[:, sub, :], in_offset=None, compute_op=ALU.add).then_inc(scattered, DMA)

            def add_zeros(n):
                if n == 0:
                    pool.wait_ge(xn_ok, NBLK)
                    pool.wait_ge(yout_free, 2 * DMA)
                    g.iota(s_idx[:, :], pattern=[[P, SUB]], base=0, channel_multiplier=1).then_inc(pool_step, 1)
                    g.memset(ybuf[:, :, :], 0.0).then_inc(pool_step, 1)
                    pool.wait_ge(pool_step, 13)
                else:
                    pool.wait_ge(scattered, n * (SUB * DMA))
                add_rows()

            def first_half(s, first, last):
                if not first:
                    outputs_low(s - 1, 1)
                first_keys(s, 1)
                if last:
                    for piece in range(PIECES):
                        pool.wait_ge(whi_ok, piece + 1)
                        low_piece(0, piece * PW)
                    add_zeros(0)

            def second_half(s, last):
                if not last:
                    first_keys(s + 1, 0)
                outputs_low(s, 0)

            first_keys(0, 0)
            first_half(0, True, False)
            with pool.Fori(0, NBLK - 2) as s:
                second_half(s, False)
                first_half(s + 1, False, False)
            second_half(NBLK - 2, False)
            first_half(NBLK - 1, False, True)
            second_half(NBLK - 1, True)
            add_zeros(1)
            outputs_low(NBLK - 1, 1)
            add_zeros(2)

            step = pool.alloc_register("pool_steps")
            pool.reg_mov(step, 13)

            def link(ins):
                ins.then_inc(pool_step, 1)
                pool.wait_ge(pool_step, pool.snap(step) + 1)
                pool.reg_add(step, step, 1)
                pool.sem_inc(pool_gate, 1)

            pool.wait_ge(tab_ok, 1)
            pool.wait_ge(table_in, DMA * NBLK)

            done = pool.alloc_register("tiles_done")
            col1 = pool.alloc_register("col1")
            col2 = pool.alloc_register("col2")
            pieces = pool.alloc_register("pieces")
            piece_col = pool.alloc_register("piece_col")
            for r in (done, col1, col2):
                pool.reg_mov(r, 0)

            def gather(col):
                n = pool.snap(done)
                pool.wait_ge(xg_free, n + 1)
                pool.wait_ge(wt_ok, n + 1)
                pool.sem_inc(pool_gate, 1)
                link(g.tensor_copy(g_idx[:, :], idx_all[:, bass.ds(col, SUB)]))
                for sub in range(SUB):
                    pool.indirect_dma_start(
                        out=xg[:, sub, :], out_offset=None, in_=table,
                        in_offset=bass.IndirectOffsetOnAxis(ap=g_idx[:, sub:sub + 1], axis=0)).then_inc(gathered, DMA)

            def scatter():
                pool.wait_ge(yout_free, DMA * (NBLK + 1))
                n = pool.snap(done)
                pool.wait_ge(ya_ok, n + 1)
                pool.wait_ge(yd_ok, n + 1)
                pool.wait_ge(scattered, (n + 1) * (SUB * DMA))
                pool.sem_inc(pool_gate, 1)
                link(g.tensor_copy(s_idx[:, :], idx_all[:, bass.ds(pool.snap(col2, min_val=0, max_val=NE * (NT // P) - SUB), SUB)]))
                add_rows()

            tiles = TileCounts(pool, n_tiles)
            with pool.Fori(0, NE // 2) as ep:
                for par in range(2):
                    pool.reg_mov(pieces, PIECES)
                    if par == 1:
                        with pool.If(ep > NE // 2 - 2):
                            pool.reg_mov(pieces, 0)
                        pool.sem_inc(pool_gate, 1)
                    n = tiles.now()
                    tiles.load_next(ep * 2 + (par + 1))
                    with pool.Fori(0, n) as j:
                        col = pool.snap(ep * (2 * NT // P) + (par * (NT // P)) + j * SUB)
                        gather(col)
                        with pool.If(pool.snap(done) > LAG - 1):
                            scatter()
                        pool.sem_inc(pool_gate, 1)
                        pool.reg_add(done, done, 1)
                        pool.reg_mov(col2, col1)
                        pool.reg_mov(col1, col)
                        with pool.If(j > 0):
                            with pool.If(j < pool.snap(pieces) + 1):
                                pool.wait_ge(whi_ok, ep * (2 * PIECES) + PIECES * (par + 1) + j)
                                pool.sem_inc(pool_gate, 1)
                                pool.reg_mov(piece_col, j * PW - PW)
                                low_piece(1 - par, pool.snap(piece_col, min_val=0, max_val=(PIECES - 1) * PW))
                            pool.sem_inc(pool_gate, 1)
                        pool.sem_inc(pool_gate, 1)
                    with pool.If(n < PIECES + 1):
                        for piece in range(PIECES):
                            with pool.If(n + PIECES - pool.snap(pieces) < piece + 2):
                                pool.wait_ge(whi_ok, ep * (2 * PIECES) + (PIECES * (par + 1) + 1 + piece))
                                pool.sem_inc(pool_gate, 1)
                                low_piece(1 - par, piece * PW)
                            pool.sem_inc(pool_gate, 1)
                    pool.sem_inc(pool_gate, 1)
                    tiles.step()
            gather(0)
            scatter()
            pool.reg_add(done, done, 1)
            pool.reg_mov(col2, col1)
            scatter()
            pool.reg_add(done, done, 1)
            pool.wait_ge(scattered, (pool.snap(done) + 1) * (SUB * DMA))

        @block.scalar
        def _(act):
            a = nc.scalar
            a.preload_act_table_set("natural_log_exp_and_others")
            def token_rstd(s):
                act.wait_ge(var_ok, s + 1)
                a.activation(ln_x[:, :], var_eps[:, :], ACT.Ln).then_inc(ln_x_ok, 1)
                act.wait_ge(ln_x_ok, s + 1)
                a.activation(rstd_x[:, :], ln_x[:, :], ACT.Exp, scale=-0.5).then_inc(rs0_ok, 1)

            def head_rstd(s, half):
                act.wait_ge(ms_ps, 2 * s + half + 1)
                a.activation(ln_o[:, half, :], ms_bank[:, :], ACT.Ln, bias=eps[:, 0:1]).then_inc(ln_o_ok, 1)
                act.wait_ge(ln_o_ok, 2 * s + half + 1)
                a.activation(rstd_o[:, half, :], ln_o[:, half, :], ACT.Exp, scale=-0.5).then_inc(ro_ok, 1)

            def heads_hi(s, half):
                act.wait_ge(on_ok, 2 * s + half + 1)
                a.activation(on_hi[:, half, :], on[:, half, :], ACT.Copy).then_inc(onhi_ok, 1)

            def front(s, banks=xt_banks):
                for c in range(KC):
                    act.wait_ge(xt_ps, KC * s + c + 1)
                    a.activation(xT_hi[:, c, :], banks[c][:, :], ACT.Copy).then_inc(xhi_ok, 1)

            def one_hot_tokens(s):
                act.wait_ge(slot_ok, s + 1)
                a.activation(oh_rhs[:, :, 0, :], oh_hi[:, :, :], ACT.Copy, scale=part[:, 0:1])
                for t in range(TT):
                    e = slice(t * NE, (t + 1) * NE)
                    last = a.activation(oh_rhs[:, e, 1, :], oh_hi[:, e, :], ACT.Copy, scale=tile_no[:, t:t + 1])
                last.then_inc(oh_ok, 1)

            def keys2(s, half):
                act.wait_ge(proj_ps, 4 * s + (1, 4)[half])
                for par in range(2):
                    a.activation(t2k[:, half, par, :], k_banks[half][1][:, :], ACT.Identity, bias=parity_b[:, par:par + 1],
                                 scale=parity[:, par:par + 1]).then_inc(t2_ok, 1)

            def queries2(s, half):
                act.wait_ge(proj_ps, 4 * s + half + 2)
                a.activation(t2q[:, half, :], q_banks[half][1][:, :], ACT.Identity, bias=bq2[:, 0:1],
                             scale=DK ** -0.5).then_inc(t2_ok, 1)

            def high_piece(par, c0):
                a.activation(w_hi[par][:, bass.ds(c0, PW)], w_raw[:, bass.ds(c0, PW)], ACT.Copy).then_inc(whi_ok, 1)

            def values_out(s, t):
                act.wait_ge(v_ps, TT * s + (1, 3, 2, 4)[t])
                a.activation(vz[:, t, :, 0:4:3, :], values_banks[t][:, 0:D].rearrange("p (g e d) -> p g e d", e=2, d=DK),
                             ACT.Copy).then_inc(v_ok, 1)

            def keys_by_token(s, half):
                act.wait_ge(kt_ps, 2 * s + half + 1)
                a.activation(k_tok[:, half, :, :].rearrange("p b m -> p (b m)"), kt_banks[half][:, 0:2 * P],
                             ACT.Copy).then_inc(kt_ok, 1)

            def squares(s, half):
                act.wait_ge(pv_ps, NGROUP * s + NGROUP // 2 * (half + 1))
                a.activation(sq[:, half, :], O[half][:, :], ACT.Square).then_inc(sq_ok, 1)

            def first_half(s, first, last):
                if not first:
                    squares(s - 1, 1)
                values_out(s, 0)
                values_out(s, 2)
                if not first:
                    head_rstd(s - 1, 1)
                    heads_hi(s - 1, 1)
                values_out(s, 1)
                values_out(s, 3)
                keys_by_token(s, 0)
                act.wait_ge(ls_ok, s + 1)
                a.activation(ex[:, :, :], ls[:, :, :], ACT.Exp).then_inc(ex_ok, 1)
                if not last:
                    token_rstd(s + 1)
                if not first:
                    one_hot_tokens(s - 1)
                queries2(s, 1)
                keys2(s, 1)
                if last:
                    act.wait_ge(w_in, DMA)
                    for piece in range(PIECES):
                        high_piece(0, piece * PW)
                keys_by_token(s, 1)
                squares(s, 0)

            def second_half(s, last):
                if not last:
                    front(s + 1)
                head_rstd(s, 0)
                if not last:
                    keys2(s + 1, 0)
                    queries2(s + 1, 0)
                heads_hi(s, 0)

            token_rstd(0)
            for f in range(4):
                if f == 2:
                    front(0, S)
                act.wait_ge(fused_ps, f + 1)
                a.activation(wqk_hi[:, f, :, :].rearrange("p c n -> p (c n)"), A[f][:, :], ACT.Copy).then_inc(setup_act, 1)
            act.wait_ge(setup_dve, 1)
            act.wait_ge(counts, 1)
            keys2(0, 0)
            queries2(0, 0)
            first_half(0, True, False)
            with act.Fori(0, NBLK - 2) as s:
                second_half(s, False)
                first_half(s + 1, False, False)
            second_half(NBLK - 2, False)
            first_half(NBLK - 1, False, True)
            second_half(NBLK - 1, True)
            squares(NBLK - 1, 1)
            head_rstd(NBLK - 1, 1)
            heads_hi(NBLK - 1, 1)
            one_hot_tokens(NBLK - 1)

            a.preload_act_table_set("silu_and_others")
            done = act.alloc_register("act_tiles")
            act.reg_mov(done, 0)
            pieces = act.alloc_register("act_pieces")
            piece_col = act.alloc_register("act_piece_col")

            def tokens_hi(n):
                act.wait_ge(xg_free, n + 2)
                a.activation(gT_hi[:, :, :].rearrange("p c t -> p (c t)"), A[0][:, :], ACT.Copy).then_inc(ghi_ok, 1)

            tokens_hi(0)
            tiles = TileCounts(act, n_tiles)
            with act.Fori(0, NE // 2) as ep:
                for par in range(2):
                    act.reg_mov(pieces, PIECES)
                    if par == 1:
                        with act.If(ep > NE // 2 - 2):
                            act.reg_mov(pieces, 0)
                        act.sem_inc(act_gate, 1)
                    n = tiles.now()
                    tiles.load_next(ep * 2 + (par + 1))

                    def next_weights():
                        act.wait_ge(yd_ok, act.snap(done) + 2)
                        act.wait_ge(w_in, (ep * 2 + (par + 2)) * DMA)
                        act.sem_inc(act_gate, 1)

                    with act.Fori(0, n) as j:
                        with act.If(j < act.snap(pieces)):
                            next_weights()
                            act.reg_mov(piece_col, j * PW)
                            high_piece(1 - par, act.snap(piece_col, min_val=0, max_val=(PIECES - 1) * PW))
                            with act.If(n < PIECES):
                                with act.If(n - j < 2):
                                    for piece in range(1, PIECES):
                                        with act.If(n < piece + 1):
                                            high_piece(1 - par, piece * PW)
                                        act.sem_inc(act_gate, 1)
                                act.sem_inc(act_gate, 1)
                            act.sem_inc(act_gate, 1)
                        act.sem_inc(act_gate, 1)
                        t = act.snap(done, min_val=0, max_val=NE * MAX_TILES - 1)
                        for ic in range(IC):
                            act.wait_ge(gu_ps, t * IC + (ic + 1))
                            a.activation(sg[:, ic, :], bank_gu(ic)[:, 0:FT], ACT.Silu).then_inc(silu_ok, 1)
                            act.wait_ge(h_free, t * IC + (ic + 1 + IC))
                            a.activation(h_hi[:, ic, :], h[:, ic, :], ACT.Copy).then_inc(hhi_ok, 1)
                        tokens_hi(t + 1)
                        act.wait_ge(y_ps, t * SUB + 1)
                        act.wait_ge(scattered, (t + 3) * (SUB * DMA))
                        a.activation(ybuf[:, 0, :], O[0][:, 0:D], ACT.Copy,
                                     scale=w_tok[:, bass.ds(t * (SUB * NE) + (ep * 2 + par), 1)]).then_inc(ya_ok, 1)
                        act.reg_add(done, done, 1)
                    tiles.step()

        @block.vector
        def _(dve):
            v = nc.vector
            chain_reg = dve.alloc_register("dve_base")
            dve.reg_mov(chain_reg, 0)

            def norm_stats(s, chain):
                dve.wait_ge(x_in, DMA * s + DMA)
                for t in range(TT):
                    last = v.bn_stats(stats[:, t, :], xa[:, t, :])
                chain.link(last)
                dve.sem_inc(dve_gate, 1)
                for t in range(TT):
                    last = v.bn_aggr(mv[:, t, :], stats[:, t, :])
                chain.link(last)
                v.tensor_scalar(var_eps[:, :], mv[:, :, 1], LN_EPS, None, ALU.add).then_inc(var_ok, 1)

            def norm_refine(s, chain):
                dve.wait_ge(rs0_ok, s + 1)
                chain.link(v.tensor_tensor(newton[:, :], rstd_x[:, :], rstd_x[:, :], ALU.mult))
                chain.link(v.tensor_tensor(newton[:, :], newton[:, :], var_eps[:, :], ALU.mult))
                chain.link(v.tensor_scalar(newton[:, :], newton[:, :], -0.5, 1.5, ALU.mult, ALU.add))
                chain.link(v.tensor_tensor(rstd_x[:, :], rstd_x[:, :], newton[:, :], ALU.mult))

            def norm_apply(s, first=False):
                if not first:
                    dve.wait_ge(table_in, DMA * s)
                    dve.wait_ge(xt_ps, KC * s)
                for t in range(TT):
                    last = v.tensor_scalar(xna[:, t, 0:D], xa[:, t, :], mv[:, t, 0:1], rstd_x[:, t:t + 1],
                                           ALU.subtract, ALU.mult)
                last.then_inc(xn_ok, 1)

            def tokens_low(s, c, banks=xt_banks):
                dve.wait_ge(xhi_ok, KC * s + c + 1)
                v.tensor_tensor(xT_lo[:, c, :], banks[c][:, :], xT_hi[:, c, :].bitcast(F32), ALU.subtract).then_inc(xlo_ok, 1)

            def logits_out(s, half):
                dve.wait_ge(v_ok, TT * s + 2 * half + 2)
                v.tensor_copy(lg[:, half, :], values_banks[half][:, D:AUG])
                v.tensor_copy(lg[:, half + 2, :], values_banks[half + 2][:, D:AUG]).then_inc(lg_ok, 1)

            def queries(s, half):
                dve.wait_ge(t2_ok, 6 * s + half + 3)
                v.scalar_tensor_tensor(q[:, half, :], q_banks[half][0][:, :], smalls[:, 4 * DK:4 * DK + 1], t2q[:, half, :],
                                       ALU.add, ALU.mult).then_inc(qk_ok, 1)

            def keys(s, half):
                for par in range(2):
                    dve.wait_ge(t2_ok, 6 * s + (1, 5)[half] + par)
                    v.scalar_tensor_tensor(kz[:, half, par, :], k_banks[half][0][:, :], smalls[:, 4 * DK + 2:4 * DK + 3],
                                           t2k[:, half, par, :], ALU.add, ALU.mult).then_inc(qk_ok, 1)

            def masked_scores(s, i):
                dve.wait_ge(s_ps, NGROUP * s + i + 1)
                v.tensor_tensor(s_sb[:, i % NS, :, :], scores_banks[i % NS][:, :].rearrange("p (n c) -> p n c", n=4),
                                causal[:, :].unsqueeze(1).to_broadcast([P, 4, P]), ALU.mult).then_inc(s_ok, 1)

            def softmax_head(s, chain):
                dve.wait_ge(lg_ok, 2 * s + 2)
                chain.link(v.tensor_reduce(mx[:, :], lg[:, :, :], axis=X_AXIS, op=ALU.max))
                v.tensor_tensor(ls[:, :, :], lg[:, :, :], mx[:, :].unsqueeze(2).to_broadcast([P, TT, NE]),
                                ALU.subtract).then_inc(ls_ok, 1)

            def softmax_tail(s, chain):
                dve.wait_ge(ex_ok, s + 1)
                chain.link(v.tensor_reduce(sm[:, :], ex[:, :, :], axis=X_AXIS, op=ALU.add))
                chain.link(v.reciprocal(sm[:, :], sm[:, :]))
                chain.link(v.tensor_tensor(pr[:, :, :], ex[:, :, :], sm[:, :].unsqueeze(2).to_broadcast([P, TT, NE]),
                                           ALU.mult))

            def choose(s, step, chain):
                pf = pr[:, :, :].unsqueeze(2).to_broadcast([P, TT, NE, NE])
                pe = pr[:, :, :].unsqueeze(3).to_broadcast([P, TT, NE, NE])
                if step == 0:
                    v.tensor_tensor(c_gt[:, :, :, :], pf, pe, ALU.is_gt)
                    chain.link(v.tensor_tensor(c_eq[:, :, :, :], pf, pe, ALU.is_equal))
                if step == 1:
                    chain.link(v.tensor_tensor(c_eq[:, :, :, :], c_eq[:, :, :, :],
                                               lower_e[:, :, :].unsqueeze(1).to_broadcast([P, TT, NE, NE]), ALU.mult))
                    chain.link(v.tensor_tensor(c_gt[:, :, :, :], c_gt[:, :, :, :], c_eq[:, :, :, :], ALU.add))
                if step == 2:
                    chain.link(v.tensor_tensor(c_gt[:, :, :, :], c_gt[:, :, :, :], pf, ALU.mult))
                    chain.link(v.tensor_reduce(cum[:, :, :], c_gt[:, :, :, :], axis=X_AXIS, op=ALU.add))
                    chain.link(v.tensor_scalar(keep[:, :, :], cum[:, :, :], TOP_P, None, ALU.is_le))
                    v.tensor_copy(sel[:, :, :], keep[:, :, :]).then_inc(sel_ok, 1)
                    v.tensor_tensor(xna[:, :, D:AUG], pr[:, :, :], keep[:, :, :], ALU.mult).then_inc(w_ok, 1)

            def slots(s, step, chain):
                if step == 0:
                    dve.wait_ge(rank_ps, s + 1)
                    for t in range(TT):
                        chain.link(v.tensor_tensor(base[:, t + 1, :], base[:, t, :],
                                                   rank_bank[:, TT * NE + t * NE:TT * NE + (t + 1) * NE], ALU.add))
                    v.tensor_tensor(slot[:, :, :], rank_bank[:, 0:TT * NE].rearrange("p (t e) -> p t e", t=TT),
                                    base[:, 0:TT, :], ALU.add).then_inc(rank_ok, 1)
                    return
                chain.link(v.tensor_scalar(keep[:, :, :], keep[:, :, :], -1.0, 1.0, ALU.mult, ALU.add))
                chain.link(v.tensor_tensor(keep[:, :, :], keep[:, :, :],
                                           from_end[:, :].unsqueeze(2).to_broadcast([P, TT, NE]), ALU.mult))
                dve.wait_ge(rank_ok, s + 1)
                chain.link(v.tensor_tensor(slot[:, :, :], slot[:, :, :], keep[:, :, :], ALU.add))
                chain.link(v.tensor_copy(slot_i[:, :, :], slot[:, :, :]))
                chain.link(v.tensor_scalar(lo_i[:, :, :], slot_i[:, :, :], P - 1, None, ALU.bitwise_and))
                chain.link(v.tensor_copy(slot_lo[:, :, :], lo_i[:, :, :]))
                chain.link(v.tensor_tensor(slot_hi[:, :, :], slot[:, :, :], slot_lo[:, :, :], ALU.subtract))
                n = TT * NE
                hi = slot_hi[:, :, :].rearrange("p t e -> p (t e)")
                v.tensor_tensor(oh_hi[:, :, :], hi_iota[:, :].unsqueeze(1).to_broadcast([P, n, NT // P]),
                                hi.unsqueeze(2).to_broadcast([P, n, NT // P]), ALU.is_equal).then_inc(slot_ok, 1)
                v.tensor_scalar(from_end[:, :], from_end[:, :], float(-BLK), None, ALU.add)
                chain.link(v.tensor_copy(base[:, 0, :], base[:, TT, :]))

            def one_hot(s, t):
                ins = v.tensor_tensor(oh_lo[:, t * NE:(t + 1) * NE, :], lo_iota[:, :].unsqueeze(1).to_broadcast([P, NE, P]),
                                      slot_lo[:, t, :].unsqueeze(2).to_broadcast([P, NE, P]), ALU.is_equal)
                if t == TT - 1:
                    ins.then_inc(lo_ok, 1)

            def head_norm(s, half, chain):
                dve.wait_ge(ro_ok, 2 * s + half + 1)
                v.tensor_tensor(on[:, half, :], O[half][:, :], rstd_o[:, half, :], ALU.mult).then_inc(on_ok, 1)

            def state(s, half):
                dve.wait_ge(kv_ps, 2 * s + half + 1)
                v.tensor_tensor(kv[:, half, :, :], kt_banks[half][:, 2 * P:4 * P].rearrange("p (n m) -> p n m", n=2),
                                head_mask[:, :, :].rearrange("p h d -> p (h d)").unsqueeze(1).to_broadcast([P, 2, P]),
                                ALU.mult).then_inc(kv_ok, 1)

            def add_residual(s, i):
                if i == 0:
                    dve.wait_ge(xr_in, DMA * s + DMA)
                    dve.wait_ge(yout_free, DMA * s + DMA)
                dve.wait_ge(wo_ps, 2 * s + i + 1)
                v.tensor_tensor(yout[:, 2 * i:2 * i + 2, :], wo_banks[i][:, :].rearrange("p (t d) -> p t d", t=2),
                                xr[:, 2 * i:2 * i + 2, :], ALU.add).then_inc(y_ok, 1)

            def add_indices(s):
                dve.wait_ge(idx_ps, s + 1)
                v.tensor_tensor(idx_acc[:, :, :, :].rearrange("p e a n -> p (e a n)"),
                                idx_bank[:, :], idx_acc[:, :, :, :].rearrange("p e a n -> p (e a n)"),
                                ALU.add).then_inc(idx_ok, 1)
                v.tensor_scalar(tile_no[:, :], tile_no[:, :], float(TT), None, ALU.add)

            def first_half(s, first, last, chain):
                logits_out(s, 0)
                masked_scores(s, 0)
                if not first:
                    one_hot(s - 1, 2)
                    one_hot(s - 1, 3)
                    head_norm(s - 1, 1, chain)
                masked_scores(s, 1)
                masked_scores(s, 2)
                if not last:
                    norm_stats(s + 1, chain)
                logits_out(s, 1)
                softmax_head(s, chain)
                softmax_tail(s, chain)
                masked_scores(s, 3)
                if not last:
                    norm_refine(s + 1, chain)
                choose(s, 0, chain)
                masked_scores(s, 4)
                state(s, 0)
                queries(s, 1)
                choose(s, 1, chain)
                masked_scores(s, 5)
                choose(s, 2, chain)
                masked_scores(s, 6)
                keys(s, 1)
                masked_scores(s, 7)
                if not first:
                    add_residual(s - 1, 0)
                if not last:
                    norm_apply(s + 1)
                masked_scores(s, 8)
                slots(s, 0, chain)
                masked_scores(s, 9)
                if not first:
                    add_residual(s - 1, 1)
                masked_scores(s, 10)
                if not first:
                    add_indices(s - 1)

            def second_half(s, last, chain):
                masked_scores(s, 11)
                state(s, 1)
                masked_scores(s, 12)
                if not last:
                    for c in range(KC):
                        tokens_low(s + 1, c)
                masked_scores(s, 13)
                if not last:
                    slots(s, 1, chain)
                    one_hot(s, 0)
                masked_scores(s, 14)
                head_norm(s, 0, chain)
                if not last:
                    keys(s + 1, 0)
                masked_scores(s, 15)
                if last:
                    slots(s, 1, chain)
                    one_hot(s, 0)
                    head_norm(s, 1, chain)
                one_hot(s, 1)
                if not last:
                    queries(s + 1, 0)

            chain = Chain(dve, dve_step, None)
            norm_stats(0, chain)
            dve.wait_ge(small_in, DMA)
            dve.wait_ge(masks, 1)
            for f in range(4):
                v.tensor_tensor(feat[:, f, :].rearrange("p (h d) -> p h d", h=HH), head_mask[:, :, :],
                                smalls[:, f * DK:(f + 1) * DK].unsqueeze(1).to_broadcast([P, HH, DK]),
                                ALU.mult).then_inc(feat_ok, 1)
            norm_refine(0, chain)
            norm_apply(0, True)
            for par in range(2):
                last = v.tensor_reduce(parity[:, par:par + 1], head_mask[:, par:HH:2, 0:1].rearrange("p h d -> p d h"),
                                       axis=X_AXIS, op=ALU.add)
            chain.link(last)
            v.tensor_scalar(parity_b[:, :], parity[:, :], smalls[:, 4 * DK + 3:4 * DK + 4], None, ALU.mult)
            v.tensor_scalar(bq2[:, :], smalls[:, 4 * DK + 1:4 * DK + 2], DK ** -0.5, None,
                            ALU.mult).then_inc(setup_dve, 1)
            for c in range(KC):
                tokens_low(0, c, S)
            for f in range(4):
                dve.wait_ge(setup_act, f + 1)
                v.tensor_tensor(wqk_lo[:, f, :, :].rearrange("p c n -> p (c n)"), A[f][:, :],
                                wqk_hi[:, f, :, :].rearrange("p c n -> p (c n)").bitcast(F32),
                                ALU.subtract).then_inc(fused_ok, 1)
            dve.wait_ge(vo_in, 2 * DMA)
            for c in range(KC):
                last = v.tensor_scalar(wo_raw[:, c, :], wo_raw[:, c, :], smalls[:, 4 * DK + 4:4 * DK + 5], None,
                                       ALU.mult)
            chain.link(last)
            v.tensor_copy(wvr_hi[:, :, :], wvr_raw)
            chain.link(v.tensor_copy(wo_hi[:, :, :], wo_raw))
            v.tensor_tensor(wvr_lo[:, :, :], wvr_raw, wvr_hi[:, :, :].bitcast(F32), ALU.subtract)
            v.tensor_tensor(wo_lo[:, :, :], wo_raw, wo_hi[:, :, :].bitcast(F32), ALU.subtract).then_inc(split_ok, 1)
            v.memset(mx[:, :], 0.0).then_inc(y_ok, 2)
            v.memset(sm[:, :], 0.0).then_inc(idx_ok, 1)
            dve.wait_ge(counts, 1)
            keys(0, 0)
            queries(0, 0)
            first_half(0, True, False, chain)
            dve.reg_mov(chain_reg, chain.n)
            with dve.Fori(0, NBLK - 2) as s:
                chain = Chain(dve, dve_step, dve.snap(chain_reg))
                second_half(s, False, chain)
                first_half(s + 1, False, False, chain)
                dve.reg_add(chain_reg, chain_reg, chain.n)
            chain = Chain(dve, dve_step, dve.snap(chain_reg))
            second_half(NBLK - 2, False, chain)
            first_half(NBLK - 1, False, True, chain)
            second_half(NBLK - 1, True, chain)
            one_hot(NBLK - 1, 2)
            one_hot(NBLK - 1, 3)
            add_indices(NBLK - 1)

            dve.wait_ge(idx_ok, NBLK + 1)
            dve.wait_ge(table_in, DMA * NBLK)
            chain.link(v.scalar_tensor_tensor(idx_f[:, :, :], idx_acc[:, :, 1, :], float(P), idx_acc[:, :, 0, :],
                                              ALU.mult, ALU.add))
            v.tensor_copy(idx_all[:, :], idx_f[:, :, :].rearrange("p e n -> p (e n)"))
            chain.link(v.tensor_scalar(cum[0:1, 0, :], base[0:1, 0, :], float(FT - 1), None, ALU.add))
            chain.link(v.tensor_copy(cnt_i[:, :], cum[0:1, 0, :]))
            chain.link(v.tensor_scalar(cnt_i[:, :], cnt_i[:, :], FT.bit_length() - 1, None, ALU.arith_shift_right))
            chain.link(v.memset(n_tiles[:, NE:NE + 1], 1))
            chain.link(v.tensor_scalar(n_tiles[:, 0:NE], cnt_i[:, :], 1, None, ALU.max))
            v.memset(h[:, :, 2:3], 0.0).then_inc(ya_ok, 2)
            v.memset(h[:, :, 0:1], 0.0).then_inc(h_free, IC)
            v.memset(h[:, :, 1:2], 0.0).then_inc(yd_ok, 2)
            v.memset(h[:, :, 3:4], 0.0).then_inc(wt_ok, 1)
            v.memset(h[:, :, 4:5], 0.0).then_inc(tab_ok, 1)
            for i in range(2):
                add_residual(NBLK - 1, i)

            done = dve.alloc_register("dve_tiles")
            dve.reg_mov(done, 0)

            def tokens_lo(n):
                dve.wait_ge(ghi_ok, n + 1)
                v.tensor_tensor(gT_lo[:, :, :].rearrange("p c t -> p (c t)"), A[0][:, :],
                                gT_hi[:, :, :].rearrange("p c t -> p (c t)").bitcast(F32), ALU.subtract).then_inc(glo_ok, 1)
                v.tensor_copy(w_tok[:, bass.ds(n * (SUB * NE), SUB * NE)].rearrange("p (a e) -> p a e", a=SUB),
                              xg[:, :, D:AUG]).then_inc(wt_ok, 1)

            tokens_lo(0)
            tiles = TileCounts(dve, n_tiles)
            with dve.Fori(0, NE // 2) as ep:
                for par in range(2):
                    n = tiles.now()
                    tiles.load_next(ep * 2 + (par + 1))
                    with dve.Fori(0, n):
                        t = dve.snap(done, min_val=0, max_val=NE * MAX_TILES - 1)
                        for ic in range(IC):
                            dve.wait_ge(silu_ok, t * IC + (ic + 1))
                            v.tensor_tensor(h[:, ic, :], sg[:, ic, :], bank_gu(ic)[:, FT:2 * FT], ALU.mult).then_inc(h_free, 1)
                            dve.wait_ge(hhi_ok, t * IC + (ic + 1))
                            v.tensor_tensor(h_lo[:, ic, :], h[:, ic, :], h_hi[:, ic, :].bitcast(F32),
                                            ALU.subtract).then_inc(hlo_ok, 1)
                        tokens_lo(t + 1)
                        dve.wait_ge(y_ps, t * SUB + 2)
                        dve.wait_ge(scattered, (t + 3) * (SUB * DMA))
                        v.tensor_scalar(ybuf[:, 1, :], O[1][:, 0:D],
                                        w_tok[:, bass.ds(t * (SUB * NE) + (NE + par) + ep * 2, 1)], None,
                                        ALU.mult).then_inc(yd_ok, 1)
                        dve.reg_add(done, done, 1)
                    tiles.step()

        @block.tensor
        def _(pe):
            mm = nc.tensor.matmul

            def product(out_ap, l_hi, l_lo, r_hi, r_lo, n, k):
                mm(out_ap, l_hi, r_hi, start=(k == 0), stop=False)
                mm(out_ap, l_hi, r_lo, start=False, stop=False)
                return mm(out_ap, l_lo, r_hi, start=False, stop=(k == n - 1))

            def transposes(s, c, banks=xt_banks):
                pe.wait_ge(xn_ok, s + 1)
                for t in range(TT):
                    last = nc.tensor.transpose(banks[c][:, t * P:(t + 1) * P], xna[:, t, c * P:(c + 1) * P], ident[:, :])
                last.then_inc(xt_ps, 1)

            def project(bank, f, half):
                w = slice(half * P, (half + 1) * P)
                for c in range(KC):
                    last = product(bank[:, :], wqk_hi[:, f, c, w], wqk_lo[:, f, c, w], xT_hi[:, c, :], xT_lo[:, c, :], KC, c)
                return last

            def values_logits(s, t):
                tok = slice(t * P, (t + 1) * P)
                for c in range(KC):
                    o = product(values_banks[t][:, 0:AUG], xT_hi[:, c, tok], xT_lo[:, c, tok],
                                wvr_hi[:, c, :], wvr_lo[:, c, :], KC, c)
                o.then_inc(v_ps, 1)

            def scores(s, i):
                half, chunk, g = group(i)
                if i == NGROUP // 2:
                    pe.wait_ge(qk_ok, 6 * s + 6)
                rows = slice(32 * g, 32 * g + 32)
                for n in range(4):
                    t, par = n // 2 * 2 + chunk, n % 2
                    tok = slice(t * P, (t + 1) * P)
                    last = mm(scores_banks[i % NS][:, n * P:(n + 1) * P], kz[rows, half, par, tok], q[rows, half, tok],
                              start=True, stop=True, tile_position=(32 * g, 0))
                last.then_inc(s_ps, 1)

            def values(s, i, first=False):
                half, chunk, g = group(i)
                if i % (NGROUP // 2) == 0 and not first:
                    pe.wait_ge(on_ok, 2 * s - 1 + half)
                if i == 0:
                    pe.wait_ge(v_ok, TT * s + 2)
                if i == PAIRS:
                    pe.wait_ge(v_ok, TT * s + TT)
                if chunk == 1 and g == 0:
                    pe.wait_ge(kv_ok, 2 * s + half + 1)
                    for b in range(2):
                        second = slice((2 * b + 1) * P, (2 * b + 2) * P)
                        mm(O[half][:, second], kv[:, half, b, :], q[:, half, second], start=False, stop=True,
                           skip_group_check=True)
                pe.wait_ge(s_ok, NGROUP * s + i + 1)
                for n in range(4):
                    t, par = n // 2 * 2 + chunk, n % 2
                    w = vz[:, t, half * PAIRS + g, 2 * par:2 * par + 2, :].rearrange("p a d -> p (a d)")
                    last = mm(O[half][32 * g:32 * g + 32, t * P:(t + 1) * P], w, s_sb[:, i % NS, n, :],
                              start=(chunk == 0 and n == 0), stop=True, skip_group_check=True, tile_position=(0, 32 * g))
                last.then_inc(pv_ps, 1)

            def mean_squares(s, half):
                pe.wait_ge(sq_ok, 2 * s + half + 1)
                mm(ms_bank[:, :], head_mean[:, :], sq[:, half, :], start=True, stop=True).then_inc(ms_ps, 1)

            def slot_tokens(s):
                pe.wait_ge(oh_ok, s + 1)
                pe.wait_ge(lo_ok, s + 1)
                for e in range(NE):
                    for t in range(TT):
                        n = t * NE + e
                        o = mm(idx_bank[:, e * 64:(e + 1) * 64], oh_lo[:, n, :],
                               oh_rhs[:, n, :, :].rearrange("p a n -> p (a n)"), start=(t == 0), stop=(t == TT - 1))
                o.then_inc(idx_ps, 1)

            def output_projection(s, i):
                pe.wait_ge(onlo_ok, 2 * s + 2)
                for t in (2 * i, 2 * i + 1):
                    tok = slice(t * P, (t + 1) * P)
                    for half in range(2):
                        o = product(wo_banks[i][:, t % 2 * D:(t % 2 + 1) * D], on_hi[:, half, tok], on_lo[:, half, tok],
                                    wo_hi[:, half, :], wo_lo[:, half, :], 2, half)
                o.then_inc(wo_ps, 1)

            def keys_by_token(s, half):
                pe.wait_ge(kf_ok, 2 * s + half + 1)
                for b in range(2):
                    o = nc.tensor.transpose(kt_banks[half][:, b * P:(b + 1) * P], kf[:, half, b, :], ident[:, :])
                o.then_inc(kt_ps, 1)

            def state(s, half):
                pe.wait_ge(kt_ok, 2 * s + half + 1)
                for b in range(2):
                    rhs = vz[:, 2 * b, half * PAIRS:(half + 1) * PAIRS, 0:4:3, :]
                    o = mm(kt_banks[half][:, (2 + b) * P:(3 + b) * P], k_tok[:, half, b, :], rhs, start=True, stop=True)
                o.then_inc(kv_ps, 1)

            def ranks(s):
                pe.wait_ge(sel_ok, s + 1)
                chosen = sel[:, :, :].rearrange("p t e -> p (t e)")
                mm(rank_bank[:, 0:TT * NE], before[:, :], chosen, start=True, stop=True)
                mm(rank_bank[:, TT * NE:2 * TT * NE], ones_bf[:, :], chosen, start=True, stop=True).then_inc(rank_ps, 1)

            def first_half(s, first):
                pe.wait_ge(qk_ok, 6 * s + 2)
                if first:
                    pe.wait_ge(split_ok, 2)
                values_logits(s, 0)
                values_logits(s, 2)
                pe.wait_ge(qk_ok, 6 * s + 3)
                scores(s, 0)
                scores(s, 1)
                if not first:
                    mean_squares(s - 1, 1)
                for i in range(NGROUP // 2 + 1):
                    values(s, i, first)
                    scores(s, i + NS)
                    if i == 0:
                        if not first:
                            pe.wait_ge(ln_o_ok, 2 * s)
                        values_logits(s, 1)
                        values_logits(s, 3)
                        pe.wait_ge(lg_ok, 2 * s + 1)
                        keys_by_token(s, 0)
                    if i == 1:
                        project(q_banks[1][0], 0, 1)
                    if i == 2:
                        pe.wait_ge(lg_ok, 2 * s + 2)
                        project(q_banks[1][1], 1, 1).then_inc(proj_ps, 1)
                        state(s, 0)
                    if i == 3:
                        project(k_banks[1][0], 2, 1)
                    if i == 4:
                        project(k_banks[1][1], 3, 1).then_inc(proj_ps, 1)
                    if i == 5 and not first:
                        pe.wait_ge(qk_ok, 6 * s + 4)
                        output_projection(s - 1, 0)
                    if i == 7:
                        if not first:
                            output_projection(s - 1, 1)
                        keys_by_token(s, 1)
                        ranks(s)
                    if i == 8:
                        state(s, 1)
                        pe.wait_ge(rank_ok, s + 1)
                        if not first:
                            slot_tokens(s - 1)

            def second_half(s, last):
                for i in range(NGROUP // 2 + 1, NGROUP):
                    values(s, i)
                    if i + NS < NGROUP:
                        scores(s, i + NS)
                    if i == 9 and not last:
                        pe.wait_ge(y_ok, 2 * s + 1)
                        transposes(s + 1, 0)
                    if i == 10:
                        if not last:
                            pe.wait_ge(idx_ok, s + 1)
                            transposes(s + 1, 1)
                        pe.wait_ge(y_ok, 2 * s + 2)
                        mean_squares(s, 0)
                    if last:
                        continue
                    if i == 11:
                        pe.wait_ge(xlo_ok, KC * s + 2 * KC)
                        project(k_banks[0][0], 2, 0)
                    if i == 12:
                        project(k_banks[0][1], 3, 0).then_inc(proj_ps, 1)
                    if i == 13:
                        pe.wait_ge(ln_o_ok, 2 * s + 1)
                        project(q_banks[0][0], 0, 0)
                    if i == 14:
                        project(q_banks[0][1], 1, 0).then_inc(proj_ps, 1)

            pe.wait_ge(natural, DMA)
            for f in range(4):
                pe.wait_ge(feat_ok, f + 1)
                for kc in range(KC):
                    for hc in range(2):
                        last = mm(A[f][:, kc * D + hc * P:kc * D + hc * P + P], nat[:, f // 2, hc, kc * P:(kc + 1) * P],
                                  feat[:, f, :], start=True, stop=True)
                last.then_inc(fused_ps, 1)
                if f == 1:
                    for c in range(KC):
                        transposes(0, c, S)
            pe.wait_ge(fused_ps, 4)
            pe.nop().then_inc(split_ok, 1)
            pe.wait_ge(fused_ok, 4)
            pe.wait_ge(xlo_ok, KC)
            for banks, f in ((k_banks[0], 2), (q_banks[0], 0)):
                project(banks[0], f, 0)
                project(banks[1], f + 1, 0).then_inc(proj_ps, 1)
            first_half(0, True)
            with pe.Fori(0, NBLK - 2) as s:
                second_half(s, False)
                first_half(s + 1, False)
            second_half(NBLK - 2, False)
            first_half(NBLK - 1, False)
            second_half(NBLK - 1, True)
            pe.wait_ge(ln_o_ok, 2 * NBLK - 1)
            mean_squares(NBLK - 1, 1)
            output_projection(NBLK - 1, 0)
            pe.wait_ge(idx_ok, NBLK)
            slot_tokens(NBLK - 1)
            pe.wait_ge(ln_o_ok, 2 * NBLK)
            output_projection(NBLK - 1, 1)

            pe.nop().then_inc(xg_free, 1)
            pe.wait_ge(tab_ok, 1)
            done = pe.alloc_register("pe_tiles")
            pe.reg_mov(done, 0)

            def tokens(n):
                pe.wait_ge(gathered, n * (SUB * DMA) + SUB * DMA)
                for c in range(KC):
                    for sub in range(SUB):
                        last = nc.tensor.transpose(A[0][:, c * FT + sub * P:c * FT + (sub + 1) * P],
                                                   xg[:, sub, c * P:(c + 1) * P], ident[:, :])
                last.then_inc(xg_free, 1)

            tokens(0)
            pe.wait_ge(y_ok, 2 * NBLK + 2)
            tiles = TileCounts(pe, n_tiles)
            with pe.Fori(0, NE // 2) as ep:
                for par in range(2):
                    n = tiles.now()
                    tiles.load_next(ep * 2 + (par + 1))
                    pe.wait_ge(wsplit, ep * (2 * PIECES) + PIECES * (par + 1))
                    pe.sem_inc(pe_gate, 1)
                    with pe.Fori(0, n):
                        t = pe.snap(done)
                        pe.wait_ge(glo_ok, t + 1)
                        for ic in range(IC):
                            pe.wait_ge(h_free, t * IC + (ic + 1))
                            for m in range(2):
                                for c in range(KC):
                                    w = slice(m * KC * NI + c * NI + ic * P, m * KC * NI + c * NI + (ic + 1) * P)
                                    last = product(bank_gu(ic)[:, m * FT:(m + 1) * FT], w_hi[par][:, w], w_lo[par][:, w],
                                                   gT_hi[:, c, :], gT_lo[:, c, :], KC, c)
                            last.then_inc(gu_ps, 1)
                        tokens(t + 1)
                        pe.wait_ge(ya_ok, t + 2)
                        pe.wait_ge(yd_ok, t + 2)
                        for ic in range(IC):
                            pe.wait_ge(hlo_ok, t * IC + (ic + 1))
                            w = slice(down0 + ic * D, down0 + (ic + 1) * D)
                            for sub in range(SUB):
                                tok = slice(sub * P, (sub + 1) * P)
                                last = product(O[sub][:, 0:D], h_hi[:, ic, tok], h_lo[:, ic, tok],
                                               w_hi[par][:, w], w_lo[par][:, w], IC, ic)
                                if ic == IC - 1:
                                    last.then_inc(y_ps, 1)
                        pe.reg_add(done, done, 1)
                    tiles.step()


def kernel(**inputs):
    import numpy as np
    import concourse.bacc as bacc
    from concourse.bass_utils import run_bass_kernel_spmd

    a = {n.replace("L0_attn_", "").replace("L0_ffn_", ""): np.asarray(v) for n, v in inputs.items()}
    by_row = lambda w: w.reshape(KC, P, -1).transpose(1, 0, 2)
    heads = lambda v: np.tile(v, (HH, 1))
    arrays = {
        "x": a["x"].reshape(NT, D),
        "wqk_nat": np.stack([by_row(a["wq"]), by_row(a["wk"])], 1),
        "small": np.concatenate([heads(a[n].T) for n in ("fq1_w", "fq2_w", "fk1_w", "fk2_w")]
                                + [heads(a[n][:, None]) for n in ("fq1_b", "fq2_b", "fk1_b", "fk2_b", "norm_w")], 1),
        "wvr": by_row(np.concatenate([a["wv"].T, a["router_w"].T], 1)),
        "wo": by_row(a["wo"].T),
        "wffn": np.concatenate([
            w.transpose(0, 2, 1).reshape(NE, -1, P, w.shape[1]).transpose(0, 2, 1, 3).reshape(NE, P, -1)
            for w in (a["gate_w"], a["up_w"], a["down_w"])], 2),
    }
    arrays = {n: np.ascontiguousarray(v) for n, v in arrays.items()}
    nc = bacc.Bacc("TRN2", target_bir_lowering=False, num_devices=1)
    args = {n: nc.dram_tensor(n, v.shape, mybir.dt.from_np(v.dtype), kind="ExternalInput").ap()
            for n, v in arrays.items()}
    out = nc.dram_tensor("out", [NT, D], F32, kind="ExternalOutput").ap()
    build(nc, out=out, **args)
    r = run_bass_kernel_spmd(nc, [arrays], core_ids=[0])
    return r.results[0]["out"].reshape(inputs["L0_attn_x"].shape)
```
